# Optimizing a Trainium2 kernel written in Bass

```python
import numpy as np
import jax
import jax.numpy as jnp

def _softmax(x, axis=-1):
    return jax.nn.softmax(x, axis=axis)

def _gelu(x):
    return jax.nn.gelu(x, approximate=True)

def _silu(x):
    return jax.nn.silu(x)

def _sigmoid(x):
    return jax.nn.sigmoid(x)

def _layernorm(x, axis=-1, eps=1e-05):
    m = jnp.mean(x, axis=axis, keepdims=True)
    v = jnp.var(x, axis=axis, keepdims=True)
    return (x - m) / jnp.sqrt(v + eps)

def _scatter_add(tgt, idx, src, axis=0):
    return tgt.at[idx].add(src)

def _segment_sum(src, seg, n):
    return jax.ops.segment_sum(src, seg, n)
kernel_name = 'mk_sandwich_d1_jaxref_r8_614a85'

def setup_inputs(seed: int=0):
    np.random.seed(seed)
    _w = jnp.asarray

    def _L0_attn_setup():
        import jax, jax.numpy as jnp
        import numpy as np
        DIM = 128
        key = jax.random.key(seed)
        kx, kw = jax.random.split(key)
        x = jax.random.normal(kx, (4, 256, DIM), dtype=jnp.float32)
        W_qkv = jax.random.normal(kw, (3 * DIM, DIM), dtype=jnp.float32) * DIM ** (-0.5)
        return {'x': x, 'W_qkv': W_qkv}
    _L0_attn_in = _L0_attn_setup()

    def _L0_ffn_setup():
        import jax, jax.numpy as jnp
        import numpy as np
        D_IN, D_HID = (128, 512)

        def _ternary(key, shape):
            return jax.random.randint(key, shape, -1, 2).astype(jnp.float32)

        def _tlin(x, w, s):
            return jnp.einsum('bsi,oi->bso', x, w) * s
        key = jax.random.key(seed)
        ks = jax.random.split(key, 12)
        inv = lambda fan: 1.0 / np.sqrt(fan).astype(np.float32)
        return {'x': jax.random.normal(ks[0], (4, 256, D_IN), dtype=jnp.float32), 'w1_w': _ternary(ks[1], (D_HID, D_IN)), 'w1_s': jax.random.uniform(ks[2], (D_HID,), dtype=jnp.float32) * inv(D_IN), 'w2_w': _ternary(ks[3], (D_HID, D_IN)), 'w2_s': jax.random.uniform(ks[4], (D_HID,), dtype=jnp.float32) * inv(D_IN), 'h1_w': _ternary(ks[5], (D_HID, D_HID)), 'h1_s': jax.random.uniform(ks[6], (D_HID,), dtype=jnp.float32) * inv(D_HID), 'h2_w': _ternary(ks[7], (D_HID, D_HID)), 'h2_s': jax.random.uniform(ks[8], (D_HID,), dtype=jnp.float32) * inv(D_HID), 'w3_w': _ternary(ks[9], (D_IN, D_HID)), 'w3_s': jax.random.uniform(ks[10], (D_IN,), dtype=jnp.float32) * inv(D_HID)}
    _L0_ffn_in = _L0_ffn_setup()
    _d = {'L0_attn_x': _L0_attn_in['x'], 'L0_attn_W_qkv': _L0_attn_in['W_qkv'], 'L0_ffn_w1_w': _L0_ffn_in['w1_w'], 'L0_ffn_w1_s': _L0_ffn_in['w1_s'], 'L0_ffn_w2_w': _L0_ffn_in['w2_w'], 'L0_ffn_w2_s': _L0_ffn_in['w2_s'], 'L0_ffn_h1_w': _L0_ffn_in['h1_w'], 'L0_ffn_h1_s': _L0_ffn_in['h1_s'], 'L0_ffn_h2_w': _L0_ffn_in['h2_w'], 'L0_ffn_h2_s': _L0_ffn_in['h2_s'], 'L0_ffn_w3_w': _L0_ffn_in['w3_w'], 'L0_ffn_w3_s': _L0_ffn_in['w3_s']}
    _x0 = _d['L0_attn_x']
    _d['L0_attn_x'] = jax.random.normal(jax.random.fold_in(jax.random.key(seed), 1), (8, 256, 128), dtype=_x0.dtype)
    del _x0
    return _d

def reference(L0_attn_x, L0_attn_W_qkv, L0_ffn_w1_w, L0_ffn_w1_s, L0_ffn_w2_w, L0_ffn_w2_s, L0_ffn_h1_w, L0_ffn_h1_s, L0_ffn_h2_w, L0_ffn_h2_s, L0_ffn_w3_w, L0_ffn_w3_s):

    def _L0_attn_ref(x, W_qkv):
        import jax, jax.numpy as jnp
        import numpy as np
        DIM = 128
        qkv = jnp.einsum('bnd,ed->bne', x, W_qkv)
        B, N, _ = qkv.shape
        qkv = qkv.reshape(B, N, 3, DIM).transpose(2, 0, 1, 3)
        q, k, v = (qkv[0], qkv[1], qkv[2])
        scale = DIM ** (-0.5)
        attn = jnp.einsum('bnd,bmd->bnm', q * scale, k)
        attn = jax.nn.softmax(attn, axis=-1)
        out = jnp.einsum('bnm,bmd->bnd', attn, v)
        return out

    def _L0_ffn_ref(x, w1_w, w1_s, w2_w, w2_s, h1_w, h1_s, h2_w, h2_s, w3_w, w3_s):
        import jax, jax.numpy as jnp
        import numpy as np
        D_IN, D_HID = (128, 512)

        def _ternary(key, shape):
            return jax.random.randint(key, shape, -1, 2).astype(jnp.float32)

        def _tlin(x, w, s):
            return jnp.einsum('bsi,oi->bso', x, w) * s
        h = jax.nn.silu(_tlin(x, w1_w, w1_s)) * _tlin(x, w2_w, w2_s)
        h = jax.nn.gelu(_tlin(h, h1_w, h1_s), approximate=False)
        h = jax.nn.gelu(_tlin(h, h2_w, h2_s), approximate=False)
        return _tlin(h, w3_w, w3_s)
    x = L0_attn_x
    x = x + _layernorm(_L0_attn_ref(_layernorm(x, axis=-1), L0_attn_W_qkv), axis=-1)
    x = x + _layernorm(_L0_ffn_ref(_layernorm(x, axis=-1), L0_ffn_w1_w, L0_ffn_w1_s, L0_ffn_w2_w, L0_ffn_w2_s, L0_ffn_h1_w, L0_ffn_h1_s, L0_ffn_h2_w, L0_ffn_h2_s, L0_ffn_w3_w, L0_ffn_w3_s), axis=-1)
    return x

_drawn_inputs = setup_inputs


def setup_inputs(seed=0):
    import zlib

    import numpy as np

    out = dict(_drawn_inputs(seed))
    spreads = {}
    factors = {}
    for name, (base, spread) in spreads.items():
        noise = np.random.default_rng([zlib.crc32(name.encode()), seed]).standard_normal(out[name].shape)
        drawn = base * np.exp(spread * noise) if base else spread * noise
        out[name] = jnp.asarray(drawn.astype(out[name].dtype))
    for name, factor in factors.items():
        out[name] = (out[name] * factor).astype(out[name].dtype)
    return out
```

```python
from contextlib import ExitStack

import numpy as np

import concourse.bass as bass
from concourse import mybir

P = 128
BATCHES, SEQ, D = 8, 256, 128
HID = 512
TILES = BATCHES * SEQ // P
TB = 4
TOK = TB * P
BLOCKS = TILES // TB
KT = HID // P
EPS = 1e-5
SCALE = float(D) ** -0.5

S_W1, S_W2, S_H1, S_H2, S_W3 = 0, KT, 2 * KT, 3 * KT, 4 * KT
N_SCALES = 4 * KT + 1


def sandwich_kernel(nc, x, w_attn, w12, h1, h2, w3, scales, out):
    f32, f32r = mybir.dt.float32, mybir.dt.float32r
    ACT, ALU = mybir.ActivationFunctionType, mybir.AluOpType
    AX = mybir.AxisListType.X

    x_view = x.rearrange("g (p j) d -> p g (j d)", j=2)
    out_view = out.rearrange("g (p j) d -> p g (j d)", j=2)

    ctx = ExitStack()
    with ctx:
        def sb(name, shape, dt=f32):
            return ctx.enter_context(nc.sbuf_tensor(name, shape, dt))

        def bank(name):
            return ctx.enter_context(nc.psum_tensor(name, [P, 512], f32))

        def sem(name):
            return ctx.enter_context(nc.semaphore(name))

        wa_raw = sb("wa_raw", [P, 3 * D])
        w12_raw = sb("w12_raw", [P, 2 * HID])
        h1_raw, h2_raw = sb("h1_raw", [P, KT, HID]), sb("h2_raw", [P, KT, HID])
        w3_raw = sb("w3_raw", [P, KT * D])
        sc = sb("sc", [P, N_SCALES])
        qk = sb("qk", [P, D])
        qk_hi, qk_lo = sb("qk_hi", [P, D], f32r), sb("qk_lo", [P, D], f32r)
        wv_hi, wv_lo = sb("wv_hi", [P, D], f32r), sb("wv_lo", [P, D], f32r)
        w12_hi, w12_lo = sb("w12_hi", [P, 2 * HID], f32r), sb("w12_lo", [P, 2 * HID], f32r)
        h1_hi, h1_lo = sb("h1_hi", [P, KT, HID], f32r), sb("h1_lo", [P, KT, HID], f32r)
        h2_hi, h2_lo = sb("h2_hi", [P, KT, HID], f32r), sb("h2_lo", [P, KT, HID], f32r)
        w3_hi, w3_lo = sb("w3_hi", [P, KT * D], f32r), sb("w3_lo", [P, KT * D], f32r)
        ident = sb("ident", [P, P])
        minus_half = sb("minus_half", [P, TB])

        xs = sb("xs", [P, TILES, D])
        x1 = sb("x1", [P, TILES, D])
        outs = sb("outs", [P, TILES, D])
        xn = sb("xn", [P, TB, D])
        xn2 = sb("xn2", [P, TB, D])
        probs = sb("probs", [P, TB, SEQ])
        y_n = sb("y_n", [P, TB, D])
        v_hi, v_lo = sb("v_hi", [P, TB, D], f32r), sb("v_lo", [P, TB, D], f32r)
        stats = sb("stats", [P, 4, TB, 6])
        mv = sb("mv", [P, 4, TB, 2])
        ve = sb("ve", [P, 4, TB])
        rstd = sb("rstd", [P, 4, TB])
        neg_max = sb("neg_max", [P, TB])
        sums = sb("sums", [P, TB])
        eps_s2 = sb("eps_s2", [P, TB])
        o_shift = sb("o_shift", [P, TILES])
        y_shift = sb("y_shift", [P, TB])
        LN_X, LN_O, LN_X1, LN_Y = range(4)

        xT_hi, xT_lo = sb("xT_hi", [P, TOK], f32r), sb("xT_lo", [P, TOK], f32r)
        gT_hi, gT_lo = sb("gT_hi", [P, TOK], f32r), sb("gT_lo", [P, TOK], f32r)
        pT_hi, pT_lo = sb("pT_hi", [P, 2, TOK], f32r), sb("pT_lo", [P, 2, TOK], f32r)
        x2T_hi, x2T_lo = sb("x2T_hi", [P, TOK], f32r), sb("x2T_lo", [P, TOK], f32r)
        silu1 = sb("silu1", [P, 2, TOK])
        act_full = sb("act_full", [P, 4, TOK])
        a1_hi, a1_lo = sb("a1_hi", [P, KT, TOK], f32r), sb("a1_lo", [P, KT, TOK], f32r)
        a2_hi, a2_lo = sb("a2_hi", [P, KT, TOK], f32r), sb("a2_lo", [P, KT, TOK], f32r)
        a3_hi, a3_lo = sb("a3_hi", [P, KT, TOK], f32r), sb("a3_lo", [P, KT, TOK], f32r)
        yT = sb("yT", [P, TOK])

        F = [bank(f"F{i}") for i in range(4)]
        A = [bank(f"A{i}") for i in range(4)]

        x_loaded = [sem(f"x_loaded{b}") for b in range(BLOCKS)]
        wa_loaded, w12_loaded, sc_loaded = sem("wa_loaded"), sem("w12_loaded"), sem("sc_loaded")
        h1_loaded, h2_loaded, w3_loaded = sem("h1_loaded"), sem("h2_loaded"), sem("w3_loaded")
        zeroed, ident_ready = sem("zeroed"), sem("ident_ready")
        qk_summed, qk_copied, qk_split, qk_ready = sem("qk_summed"), sem("qk_copied"), sem("qk_split"), sem("qk_ready")
        wv_split, wv_ready = sem("wv_split"), sem("wv_ready")
        w12_split, w12_ready = sem("w12_split"), sem("w12_ready")
        h1_split, h1_ready = sem("h1_split"), sem("h1_ready")
        h2_split, h2_ready = sem("h2_split"), sem("h2_ready")
        w3_split, w3_ready = sem("w3_split"), sem("w3_ready")
        chain = sem("vector_chain")
        var_ready = [sem(f"var_ready{i}") for i in range(4)]
        rstd_ready = [sem(f"rstd_ready{i}") for i in range(4)]
        xn_ready, xT_in_psum, xT_hi_ready, xT_ready = sem("xn_ready"), sem("xT_in_psum"), sem("xT_hi_ready"), sem("xT_ready")
        gT_in_psum, gT_hi_ready, gT_ready = sem("gT_in_psum"), sem("gT_hi_ready"), sem("gT_ready")
        v_in_psum, v_hi_ready, v_ready = sem("v_in_psum"), sem("v_hi_ready"), sem("v_ready")
        scores_ready, max_ready, probs_ready, sums_ready = sem("scores_ready"), sem("max_ready"), sem("probs_ready"), sem("sums_ready")
        pT_in_psum, pT_hi_ready, pT_ready = sem("pT_in_psum"), sem("pT_hi_ready"), sem("pT_ready")
        o_in_psum, x1_ready, xn2_ready = sem("o_in_psum"), sem("x1_ready"), sem("xn2_ready")
        x2T_in_psum, x2T_hi_ready, x2T_ready = sem("x2T_in_psum"), sem("x2T_hi_ready"), sem("x2T_ready")
        up_in_psum, silu_ready, a1_full, a1_hi_ready, a1_ready = sem("up_in_psum"), sem("silu_ready"), sem("a1_full"), sem("a1_hi_ready"), sem("a1_ready")
        h1_in_psum, a2_full, a2_hi_ready, a2_ready = sem("h1_in_psum"), sem("a2_full"), sem("a2_hi_ready"), sem("a2_ready")
        h2_in_psum, a3_full, a3_hi_ready, a3_ready = sem("h2_in_psum"), sem("a3_full"), sem("a3_hi_ready"), sem("a3_ready")
        yT_in_psum, yT_ready, y_in_psum = sem("yT_in_psum"), sem("yT_ready"), sem("y_in_psum")
        y_shift_ready, yn_ready, out_ready, out_stored = sem("y_shift_ready"), sem("yn_ready"), sem("out_ready"), sem("out_stored")

        block = ctx.enter_context(nc.Block())

        @block.sync
        def _(sp):
            def load_x(b):
                sp.dma_start(xs[:, TB * b:TB * (b + 1), :].rearrange("p (g j) d -> p g (j d)", j=2),
                             x_view[:, 2 * b:2 * b + 2, :]).then_inc(x_loaded[b], 16)

            load_x(0)
            sp.dma_start(wa_raw[:, :], w_attn).then_inc(wa_loaded, 16)
            load_x(1)
            sp.dma_start(w12_raw[:, :], w12).then_inc(w12_loaded, 16)
            sp.dma_start(sc[:, :], scales).then_inc(sc_loaded, 16)
            sp.dma_start(h1_raw[:, :, :], h1.rearrange("(k p) o -> p k o", p=P)).then_inc(h1_loaded, 16)
            load_x(2)
            sp.dma_start(h2_raw[:, :, :], h2.rearrange("(k p) o -> p k o", p=P)).then_inc(h2_loaded, 16)
            load_x(3)
            sp.dma_start(w3_raw[:, :], w3).then_inc(w3_loaded, 16)
            for b in range(BLOCKS):
                sp.wait_ge(out_ready, b + 1)
                sp.dma_start(out_view[:, 2 * b:2 * b + 2, :],
                             outs[:, TB * b:TB * (b + 1), :].rearrange("p (g j) d -> p g (j d)", j=2)).then_inc(out_stored, 16)
            sp.wait_ge(out_stored, 16 * BLOCKS)

        @block.gpsimd
        def _(pool):
            nc.gpsimd.memset(ident[:, :], 0.0).then_inc(zeroed, 1)
            nc.gpsimd.memset(minus_half[:, :], -0.5).then_inc(zeroed, 1)
            pool.wait_ge(zeroed, 2)
            nc.gpsimd.affine_select(out=ident[:, :], in_=ident[:, :], compare_op=ALU.not_equal, fill=1.0, base=0,
                                    pattern=[[-1, P]], channel_multiplier=1).then_inc(ident_ready, 1)

            def rsqrt(ln, b):
                pool.wait_ge(var_ready[ln], b + 1)
                nc.gpsimd.tensor_tensor(rstd[:, ln, :], ve[:, ln, :], minus_half[:, :], ALU.pow).then_inc(rstd_ready[ln], 1)

            def split_weights(raw, hi, loaded, split):
                pool.wait_ge(loaded, 16)
                nc.gpsimd.tensor_copy(hi, raw).then_inc(split, 1)

            def hi_part(b, o, full, dst, full_sem, hi_sem, used_sem, uses):
                if b > 0 and o == 0:
                    pool.wait_ge(used_sem, uses * b)
                pool.wait_ge(full_sem, KT * b + o + 1)
                nc.gpsimd.tensor_copy(dst[:, o, :], full).then_inc(hi_sem, 1)

            def last_add(b):
                pool.wait_ge(yn_ready, TB * (b + 1))
                pool.wait_ge(x1_ready, b + 1)
                nc.gpsimd.tensor_tensor(outs[:, TB * b:TB * (b + 1), :], y_n[:, :, :],
                                        x1[:, TB * b:TB * (b + 1), :], ALU.add).then_inc(out_ready, 1)

            rsqrt(LN_X, 0)
            rsqrt(LN_X, 1)
            for k in range(KT):
                split_weights(h1_raw[:, k, :], h1_hi[:, k, :], h1_loaded, h1_split)
            rsqrt(LN_O, 0)
            rsqrt(LN_X1, 0)
            for k in range(KT):
                split_weights(h2_raw[:, k, :], h2_hi[:, k, :], h2_loaded, h2_split)
            split_weights(w3_raw[:, :], w3_hi[:, :], w3_loaded, w3_split)
            for o in range(KT):
                hi_part(0, o, act_full[:, o, :], a1_hi, a1_full, a1_hi_ready, h1_in_psum, KT)
            for b in range(BLOCKS):
                for o in range(2):
                    hi_part(b, o, act_full[:, o, :], a2_hi, a2_full, a2_hi_ready, h2_in_psum, KT)
                if b + 1 < BLOCKS:
                    rsqrt(LN_O, b + 1)
                    rsqrt(LN_X1, b + 1)
                for o in range(2, KT):
                    hi_part(b, o, act_full[:, o, :], a2_hi, a2_full, a2_hi_ready, h2_in_psum, KT)
                if b + 2 < BLOCKS:
                    rsqrt(LN_X, b + 2)
                for o in range(KT):
                    hi_part(b, o, act_full[:, o, :], a3_hi, a3_full, a3_hi_ready, yT_in_psum, 1)
                if b + 1 < BLOCKS:
                    for o in range(KT):
                        hi_part(b + 1, o, act_full[:, o, :], a1_hi, a1_full, a1_hi_ready, h1_in_psum, KT)
                rsqrt(LN_Y, b)
                last_add(b)

        @block.scalar
        def _(act):
            def hi_from_psum(dst, src, ready, n, done):
                act.wait_ge(ready, n)
                nc.scalar.activation(dst, src, ACT.Copy).then_inc(done, 1)

            def exps(b):
                for t in range(TB):
                    g, j = divmod(t, 2)
                    if j == 0:
                        act.wait_ge(max_ready, 2 * b + g + 1)
                    if b > 0 and t == 0:
                        act.wait_ge(pT_in_psum, 2 * b)
                        act.wait_ge(x1_ready, b)
                    nc.scalar.activation(probs[:, t, :], S_BANK[g][:, j * SEQ:(j + 1) * SEQ], ACT.Exp,
                                         bias=neg_max[:, t:t + 1], accum_out=sums[:, t:t + 1]).then_inc(probs_ready, 1)

            def front(b, part):
                if part == 0:
                    if b > 0:
                        act.wait_ge(scores_ready, 2 * b)
                    hi_from_psum(xT_hi[:, :], A[0][:, :], xT_in_psum, b + 1, xT_hi_ready)
                else:
                    hi_from_psum(gT_hi[:, :], A[1][:, :], gT_in_psum, b + 1, gT_hi_ready)
                    if b > 0:
                        act.wait_ge(o_in_psum, b)
                    hi_from_psum(v_hi[:, :, :], A[2][:, :], v_in_psum, b + 1, v_hi_ready)

            def probs_hi(b):
                for g in range(2):
                    if b > 0 and g == 0:
                        act.wait_ge(o_in_psum, b)
                    hi_from_psum(pT_hi[:, g, :], PT_BANK[g][:, :], pT_in_psum, 2 * b + g + 1, pT_hi_ready)

            def x2T(b):
                if b > 0:
                    act.wait_ge(up_in_psum, KT * b)
                hi_from_psum(x2T_hi[:, :], A[3][:, :], x2T_in_psum, b + 1, x2T_hi_ready)

            def silus(b):
                for o in range(KT):
                    act.wait_ge(up_in_psum, KT * b + o + 1)
                    if KT * b + o >= 2:
                        act.wait_ge(a1_full, KT * b + o - 1)
                    nc.scalar.activation(silu1[:, o % 2, :], F[2 * (o % 2)][:, :], ACT.Silu,
                                         scale=sc[:, S_W1 + o:S_W1 + o + 1]).then_inc(silu_ready, 1)

            def gelu(b, o, first_scale, in_psum, slot_free, done):
                act.wait_ge(in_psum, KT * b + o + 1)
                act.wait_ge(slot_free, KT * b + o + 1)
                nc.scalar.activation(act_full[:, o, :], F[o][:, :], ACT.Gelu,
                                     scale=sc[:, first_scale + o:first_scale + o + 1]).then_inc(done, 1)

            def finish(b):
                act.wait_ge(yT_in_psum, b + 1)
                if b > 0:
                    act.wait_ge(y_in_psum, b)
                nc.scalar.activation(yT[:, :], A[1][:, :], ACT.Copy, scale=sc[:, S_W3:S_W3 + 1]).then_inc(yT_ready, 1)
                act.wait_ge(y_shift_ready, b + 1)
                if b > 0:
                    act.wait_ge(out_ready, b)
                for t in range(TB):
                    nc.scalar.activation(y_n[:, t, :], A[2][:, t * D:(t + 1) * D], ACT.Identity,
                                         bias=y_shift[:, t:t + 1], scale=rstd[:, LN_Y, t:t + 1]).then_inc(yn_ready, 1)

            S_BANK = (A[3], A[0])
            PT_BANK = (A[3], A[1])

            act.wait_ge(qk_summed, 1)
            nc.scalar.activation(qk[:, :], F[0][:, 0:D], ACT.Copy, scale=SCALE).then_inc(qk_copied, 1)
            act.wait_ge(w12_loaded, 16)
            nc.scalar.activation(w12_hi[:, :], w12_raw[:, :], ACT.Copy).then_inc(w12_split, 1)
            act.wait_ge(sc_loaded, 16)
            front(0, 0)
            front(0, 1)
            exps(0)
            probs_hi(0)
            x2T(0)
            front(1, 0)
            front(1, 1)
            silus(0)
            for b in range(BLOCKS):
                if b + 1 < BLOCKS:
                    exps(b + 1)
                    probs_hi(b + 1)
                for o in range(KT):
                    gelu(b, o, S_H1, h1_in_psum, a1_ready, a2_full)
                if b + 1 < BLOCKS:
                    x2T(b + 1)
                gelu(b, 0, S_H2, h2_in_psum, a2_ready, a3_full)
                if b + 2 < BLOCKS:
                    front(b + 2, 0)
                gelu(b, 1, S_H2, h2_in_psum, a2_ready, a3_full)
                if b + 2 < BLOCKS:
                    front(b + 2, 1)
                gelu(b, 2, S_H2, h2_in_psum, a2_ready, a3_full)
                gelu(b, 3, S_H2, h2_in_psum, a2_ready, a3_full)
                if b + 1 < BLOCKS:
                    silus(b + 1)
                finish(b)

        @block.vector
        def _(dve):
            links = [0]

            def link(ins):
                links[0] += 1
                ins.then_inc(chain, 1)
                dve.wait_ge(chain, links[0])

            def lo_part(dst, full, hi, hi_sem, n, done):
                dve.wait_ge(hi_sem, n)
                nc.vector.tensor_tensor(dst, full, hi.bitcast(f32), ALU.subtract).then_inc(done, 1)

            def statistics(ln, tiles):
                for t in range(TB):
                    last = nc.vector.bn_stats(stats[:, ln, t, :], tiles(t))
                link(last)
                for t in range(TB):
                    last = nc.vector.bn_aggr(mv[:, ln, t, :], stats[:, ln, t, :])
                link(last)

            def x_norm(b):
                if b > 0:
                    dve.wait_ge(xT_in_psum, b)
                dve.wait_ge(x_loaded[b], 16)
                statistics(LN_X, lambda t: xs[:, TB * b + t, :])
                nc.vector.tensor_scalar(ve[:, LN_X, :], mv[:, LN_X, :, 1], EPS, None, ALU.add).then_inc(var_ready[LN_X], 1)
                normalise(b, LN_X, lambda t: xs[:, TB * b + t, :], xn, xn_ready)

            def normalise(b, ln, src, dst, done):
                dve.wait_ge(rstd_ready[ln], b + 1)
                for t in range(TB):
                    nc.vector.tensor_scalar(dst[:, t, :], src(t), mv[:, ln, t, 0:1], rstd[:, ln, t:t + 1],
                                            ALU.subtract, ALU.mult).then_inc(done, 1)

            def maxima(b):
                for g, s in enumerate((A[3], A[0])):
                    dve.wait_ge(scores_ready, 2 * b + g + 1)
                    if b > 0 and g == 0:
                        dve.wait_ge(probs_ready, TB * b)
                    nc.vector.tensor_reduce(neg_max[:, 2 * g:2 * g + 2], s[:, :].rearrange("p (j m) -> p j m", j=2),
                                            AX, ALU.max, negate=True).then_inc(max_ready, 1)

            def xT_part(b):
                lo_part(xT_lo[:, :], A[0][:, :], xT_hi[:, :], xT_hi_ready, b + 1, xT_ready)

            def gv_part(b):
                lo_part(gT_lo[:, :], A[1][:, :], gT_hi[:, :], gT_hi_ready, b + 1, gT_ready)
                lo_part(v_lo[:, :, :], A[2][:, :].rearrange("p (t d) -> p t d", t=TB), v_hi[:, :, :], v_hi_ready, b + 1, v_ready)

            def probs_lo(b):
                dve.wait_ge(probs_ready, TB * (b + 1))
                nc.vector.scalar_tensor_tensor(eps_s2[:, :], sums[:, :], EPS, sums[:, :], ALU.mult, ALU.mult).then_inc(sums_ready, 1)
                for g, s in enumerate((A[3], A[1])):
                    lo_part(pT_lo[:, g, :], s[:, :], pT_hi[:, g, :], pT_hi_ready, 2 * b + g + 1, pT_ready)

            def attention_out(b):
                dve.wait_ge(o_in_psum, b + 1)
                o = lambda t: A[2][:, t * D:(t + 1) * D]
                statistics(LN_O, o)
                dve.wait_ge(sums_ready, b + 1)
                nc.vector.tensor_tensor(ve[:, LN_O, :], mv[:, LN_O, :, 1], eps_s2[:, :], ALU.add).then_inc(var_ready[LN_O], 1)
                dve.wait_ge(rstd_ready[LN_O], b + 1)
                for t in range(TB):
                    last = nc.vector.scalar_tensor_tensor(x1[:, TB * b + t, :], o(t), rstd[:, LN_O, t:t + 1], xs[:, TB * b + t, :],
                                                          ALU.mult, ALU.add)
                last.then_inc(x1_ready, 1)
                nc.vector.tensor_tensor(o_shift[:, TB * b:TB * (b + 1)], mv[:, LN_O, :, 0], rstd[:, LN_O, :], ALU.mult)
                dve.wait_ge(x1_ready, b + 1)
                x1t = lambda t: x1[:, TB * b + t, :]
                statistics(LN_X1, x1t)
                nc.vector.tensor_scalar(ve[:, LN_X1, :], mv[:, LN_X1, :, 1], EPS, None, ALU.add).then_inc(var_ready[LN_X1], 1)
                if b > 0:
                    dve.wait_ge(x2T_in_psum, b)
                normalise(b, LN_X1, x1t, xn2, xn2_ready)

            def x2T_part(b):
                lo_part(x2T_lo[:, :], A[3][:, :], x2T_hi[:, :], x2T_hi_ready, b + 1, x2T_ready)

            def gated(b, o):
                dve.wait_ge(silu_ready, KT * b + o + 1)
                if b > 0:
                    dve.wait_ge(a3_ready, KT * (b - 1) + o + 1)
                nc.vector.scalar_tensor_tensor(act_full[:, o, :], F[2 * (o % 2) + 1][:, :], sc[:, S_W2 + o:S_W2 + o + 1],
                                               silu1[:, o % 2, :], ALU.mult, ALU.mult).then_inc(a1_full, 1)

            def act_lo(b, o, dst, hi, hi_sem, done):
                lo_part(dst[:, o, :], act_full[:, o, :], hi[:, o, :], hi_sem, KT * b + o + 1, done)

            def gates(b):
                gated(b, 0)
                for o in range(1, KT):
                    gated(b, o)
                    act_lo(b, o - 1, a1_lo, a1_hi, a1_hi_ready, a1_ready)
                act_lo(b, KT - 1, a1_lo, a1_hi, a1_hi_ready, a1_ready)

            def y_norm(b):
                dve.wait_ge(y_in_psum, b + 1)
                if b > 0:
                    dve.wait_ge(yn_ready, TB * b)
                statistics(LN_Y, lambda t: A[2][:, t * D:(t + 1) * D])
                nc.vector.tensor_scalar(ve[:, LN_Y, :], mv[:, LN_Y, :, 1], EPS, None, ALU.add).then_inc(var_ready[LN_Y], 1)
                dve.wait_ge(rstd_ready[LN_Y], b + 1)
                link(nc.vector.tensor_tensor(y_shift[:, :], mv[:, LN_Y, :, 0], rstd[:, LN_Y, :], ALU.mult))
                nc.vector.scalar_tensor_tensor(y_shift[:, :], y_shift[:, :], -1.0, o_shift[:, TB * b:TB * (b + 1)],
                                               ALU.mult, ALU.subtract).then_inc(y_shift_ready, 1)

            def weights_lo(dst, raw, hi, split, n, done):
                lo_part(dst, raw, hi, split, n, done)

            dve.wait_ge(wa_loaded, 16)
            nc.vector.tensor_copy(wv_hi[:, :], wa_raw[:, 2 * D:3 * D]).then_inc(wv_split, 1)
            lo_part(wv_lo[:, :], wa_raw[:, 2 * D:3 * D], wv_hi[:, :], wv_split, 1, wv_ready)
            x_norm(0)
            dve.wait_ge(qk_copied, 1)
            nc.vector.tensor_copy(qk_hi[:, :], qk[:, :]).then_inc(qk_split, 1)
            lo_part(qk_lo[:, :], qk[:, :], qk_hi[:, :], qk_split, 1, qk_ready)
            xT_part(0)
            gv_part(0)
            maxima(0)
            x_norm(1)
            lo_part(w12_lo[:, :], w12_raw[:, :], w12_hi[:, :], w12_split, 1, w12_ready)
            probs_lo(0)
            for k in range(KT):
                lo_part(h1_lo[:, k, :], h1_raw[:, k, :], h1_hi[:, k, :], h1_split, k + 1, h1_ready)
            attention_out(0)
            x2T_part(0)
            xT_part(1)
            gv_part(1)
            maxima(1)
            gates(0)
            for k in range(KT):
                lo_part(h2_lo[:, k, :], h2_raw[:, k, :], h2_hi[:, k, :], h2_split, k + 1, h2_ready)
            lo_part(w3_lo[:, :], w3_raw[:, :], w3_hi[:, :], w3_split, 1, w3_ready)
            for b in range(BLOCKS):
                if b + 1 < BLOCKS:
                    probs_lo(b + 1)
                act_lo(b, 0, a2_lo, a2_hi, a2_hi_ready, a2_ready)
                act_lo(b, 1, a2_lo, a2_hi, a2_hi_ready, a2_ready)
                if b + 1 < BLOCKS:
                    attention_out(b + 1)
                act_lo(b, 2, a2_lo, a2_hi, a2_hi_ready, a2_ready)
                act_lo(b, 3, a2_lo, a2_hi, a2_hi_ready, a2_ready)
                if b + 1 < BLOCKS:
                    x2T_part(b + 1)
                if b + 2 < BLOCKS:
                    x_norm(b + 2)
                act_lo(b, 0, a3_lo, a3_hi, a3_hi_ready, a3_ready)
                if b + 2 < BLOCKS:
                    xT_part(b + 2)
                act_lo(b, 1, a3_lo, a3_hi, a3_hi_ready, a3_ready)
                if b + 2 < BLOCKS:
                    gv_part(b + 2)
                act_lo(b, 2, a3_lo, a3_hi, a3_hi_ready, a3_ready)
                if b + 2 < BLOCKS:
                    maxima(b + 2)
                act_lo(b, 3, a3_lo, a3_hi, a3_hi_ready, a3_ready)
                if b + 1 < BLOCKS:
                    gates(b + 1)
                y_norm(b)

        @block.tensor
        def _(pe):
            def product(out, terms):
                last = None
                for n, (w_hi, w_lo, x_hi, x_lo) in enumerate(terms):
                    for m, (w, v) in enumerate(((w_hi, x_hi), (w_hi, x_lo), (w_lo, x_hi))):
                        last = nc.tensor.matmul(out, w, v, start=(n == 0 and m == 0), stop=(n == len(terms) - 1 and m == 2))
                return last

            def front_transposes(b):
                pe.wait_ge(xn_ready, TB * (b + 1))
                if b > 0:
                    pe.wait_ge(probs_ready, TB * b)
                for t in range(TB):
                    last = nc.tensor.transpose(A[0][:, t * P:(t + 1) * P], xn[:, t, :], ident[:, :])
                last.then_inc(xT_in_psum, 1)

            def front_projections(b):
                pe.wait_ge(xT_ready, b + 1)
                if b > 0:
                    pe.wait_ge(pT_ready, 2 * b)
                else:
                    pe.wait_ge(qk_ready, 1)
                    pe.wait_ge(wv_ready, 1)
                product(A[1][:, :], [(qk_hi[:, :], qk_lo[:, :], xT_hi[:, :], xT_lo[:, :])]).then_inc(gT_in_psum, 1)
                if b > 0:
                    pe.wait_ge(x1_ready, b)
                for t in range(TB):
                    c = slice(t * P, (t + 1) * P)
                    last = product(A[2][:, c], [(xT_hi[:, c], xT_lo[:, c], wv_hi[:, :], wv_lo[:, :])])
                last.then_inc(v_in_psum, 1)

            def front_scores(b):
                pe.wait_ge(gT_ready, b + 1)
                if b > 0:
                    pe.wait_ge(x2T_ready, b)
                for g, s in enumerate((A[3], A[0])):
                    keys = slice(g * SEQ, (g + 1) * SEQ)
                    for j in range(2):
                        c = slice((2 * g + j) * P, (2 * g + j + 1) * P)
                        last = product(s[:, j * SEQ:(j + 1) * SEQ], [(gT_hi[:, c], gT_lo[:, c], xT_hi[:, keys], xT_lo[:, keys])])
                    last.then_inc(scores_ready, 1)

            def probs_transposes(b):
                for g, s in enumerate((A[3], A[1])):
                    pe.wait_ge(probs_ready, TB * b + 2 * g + 2)
                    if g == 0:
                        pe.wait_ge(ident_ready, 1)
                    elif b >= 2:
                        pe.wait_ge(yT_ready, b - 1)
                    elif b == 0:
                        pe.wait_ge(gT_ready, 1)
                    for h in range(2):
                        for j in range(2):
                            c = (2 * h + j) * P
                            last = nc.tensor.transpose(s[:, c:c + P], probs[:, 2 * g + j, h * P:(h + 1) * P], ident[:, :])
                    last.then_inc(pT_in_psum, 1)

            def attend(b):
                pe.wait_ge(v_ready, b + 1)
                if b >= 2:
                    pe.wait_ge(yn_ready, TB * (b - 1))
                for t in range(TB):
                    g, j = divmod(t, 2)
                    if j == 0:
                        pe.wait_ge(pT_ready, 2 * b + g + 1)
                    last = product(A[2][:, t * D:(t + 1) * D],
                                   [(pT_hi[:, g, (2 * h + j) * P:(2 * h + j + 1) * P], pT_lo[:, g, (2 * h + j) * P:(2 * h + j + 1) * P],
                                     v_hi[:, 2 * g + h, :], v_lo[:, 2 * g + h, :]) for h in range(2)])
                last.then_inc(o_in_psum, 1)

            def x2_transposes(b):
                pe.wait_ge(pT_ready, 2 * b + 1)
                pe.wait_ge(xn2_ready, TB * (b + 1))
                for t in range(TB):
                    last = nc.tensor.transpose(A[3][:, t * P:(t + 1) * P], xn2[:, t, :], ident[:, :])
                last.then_inc(x2T_in_psum, 1)

            def up(b):
                pe.wait_ge(x2T_ready, b + 1)
                if b == 0:
                    pe.wait_ge(w12_ready, 1)
                for o in range(KT):
                    if o >= 2:
                        pe.wait_ge(a1_full, KT * b + o - 1)
                    elif b > 0:
                        pe.wait_ge(a3_full, KT * (b - 1) + 2 * o + 2)
                    for m in range(2):
                        c = slice(m * HID + o * P, m * HID + (o + 1) * P)
                        last = product(F[2 * (o % 2) + m][:, :], [(w12_hi[:, c], w12_lo[:, c], x2T_hi[:, :], x2T_lo[:, :])])
                    last.then_inc(up_in_psum, 1)

            def hidden(b, o, w_hi, w_lo, x_hi, x_lo, x_sem, w_sem, bank_sem, bank_n, done):
                if b == 0 and o == 0:
                    pe.wait_ge(w_sem, KT)
                pe.wait_ge(bank_sem, bank_n)
                if o == 0:
                    pe.wait_ge(x_sem, KT * (b + 1))
                c = slice(o * P, (o + 1) * P)
                product(F[o][:, :], [(w_hi[:, k, c], w_lo[:, k, c], x_hi[:, k, :], x_lo[:, k, :]) for k in range(KT)]).then_inc(done, 1)

            def down(b):
                pe.wait_ge(a3_ready, KT * (b + 1))
                if b == 0:
                    pe.wait_ge(w3_ready, 1)
                pe.wait_ge(gT_ready, min(b + 3, BLOCKS))
                product(A[1][:, :], [(w3_hi[:, k * D:(k + 1) * D], w3_lo[:, k * D:(k + 1) * D], a3_hi[:, k, :], a3_lo[:, k, :])
                                     for k in range(KT)]).then_inc(yT_in_psum, 1)

            def y_transposes(b):
                pe.wait_ge(yT_ready, b + 1)
                pe.wait_ge(v_ready, min(b + 3, BLOCKS))
                for t in range(TB):
                    last = nc.tensor.transpose(A[2][:, t * P:(t + 1) * P], yT[:, t * P:(t + 1) * P], ident[:, :])
                last.then_inc(y_in_psum, 1)

            def h1_layer(b, o):
                hidden(b, o, h1_hi, h1_lo, a1_hi, a1_lo, a1_ready, h1_ready, a1_full, KT * b + 3 + o // 2, h1_in_psum)

            def h2_layer(b, o):
                hidden(b, o, h2_hi, h2_lo, a2_hi, a2_lo, a2_ready, h2_ready, a2_full, KT * b + o + 1, h2_in_psum)

            pe.wait_ge(wa_loaded, 16)
            nc.tensor.matmul(F[0][:, 0:D], wa_raw[:, 0:D], wa_raw[:, D:2 * D], start=True, stop=True).then_inc(qk_summed, 1)
            pe.wait_ge(ident_ready, 1)
            front_transposes(0)
            front_projections(0)
            front_scores(0)
            probs_transposes(0)
            attend(0)
            x2_transposes(0)
            front_transposes(1)
            front_projections(1)
            front_scores(1)
            pe.wait_ge(qk_copied, 1)
            up(0)
            for b in range(BLOCKS):
                h1_layer(b, 0)
                if b + 1 < BLOCKS:
                    probs_transposes(b + 1)
                h1_layer(b, 1)
                if b + 1 < BLOCKS:
                    attend(b + 1)
                h1_layer(b, 2)
                h1_layer(b, 3)
                if b + 1 < BLOCKS:
                    x2_transposes(b + 1)
                h2_layer(b, 0)
                if b + 2 < BLOCKS:
                    front_transposes(b + 2)
                h2_layer(b, 1)
                if b + 2 < BLOCKS:
                    front_projections(b + 2)
                h2_layer(b, 2)
                if b + 2 < BLOCKS:
                    front_scores(b + 2)
                h2_layer(b, 3)
                if b + 1 < BLOCKS:
                    up(b + 1)
                down(b)
                y_transposes(b)


def kernel(**inputs):
    import concourse.bacc as bacc
    from concourse.bass_utils import run_bass_kernel_spmd

    a = {name: np.asarray(value) for name, value in inputs.items()}
    w_qkv = a["L0_attn_W_qkv"]
    arrays = {
        "x": a["L0_attn_x"],
        "w_attn": np.concatenate([w_qkv[:D], w_qkv[D:2 * D], w_qkv[2 * D:].T], axis=1),
        "w12": np.concatenate([a["L0_ffn_w1_w"].T, a["L0_ffn_w2_w"].T], axis=1),
        "h1": a["L0_ffn_h1_w"].T,
        "h2": a["L0_ffn_h2_w"].T,
        "w3": a["L0_ffn_w3_w"].T.reshape(KT, P, D).transpose(1, 0, 2).reshape(P, KT * D),
        "scales": np.concatenate([a["L0_ffn_" + n].reshape(-1, P) for n in ("w1_s", "w2_s", "h1_s", "h2_s", "w3_s")]).T,
    }
    arrays = {name: np.ascontiguousarray(value) for name, value in arrays.items()}
    nc = bacc.Bacc("TRN2", target_bir_lowering=False, num_devices=1)
    args = [nc.dram_tensor(name, v.shape, mybir.dt.from_np(v.dtype), kind="ExternalInput").ap() for name, v in arrays.items()]
    out = nc.dram_tensor("out", (BATCHES, SEQ, D), mybir.dt.float32, kind="ExternalOutput").ap()
    sandwich_kernel(nc, *args, out)
    result = run_bass_kernel_spmd(nc, [arrays], core_ids=[0])
    return result.results[0]["out"]
```

```python
from contextlib import ExitStack

import numpy as np

import concourse.bass as bass
from concourse import mybir

P = 128
BATCHES, SEQ, D = 8, 256, 128
HID = 512
TILES = BATCHES * SEQ // P
TB = 4
TOK = TB * P
BLOCKS = TILES // TB
KT = HID // P
EPS = 1e-5
SCALE = float(D) ** -0.5

S_W1, S_W2, S_H1, S_H2, S_W3 = 0, KT, 2 * KT, 3 * KT, 4 * KT
N_SCALES = 4 * KT + 1


def sandwich_kernel(nc, x, w_attn, w12, h1, h2, w3, scales, out):
    f32, f32r = mybir.dt.float32, mybir.dt.float32r
    ACT, ALU = mybir.ActivationFunctionType, mybir.AluOpType
    AX = mybir.AxisListType.X

    x_view = x.rearrange("g (p j) d -> p g (j d)", j=2)
    out_view = out.rearrange("g (p j) d -> p g (j d)", j=2)

    ctx = ExitStack()
    with ctx:
        def sb(name, shape, dt=f32):
            return ctx.enter_context(nc.sbuf_tensor(name, shape, dt))

        def bank(name):
            return ctx.enter_context(nc.psum_tensor(name, [P, 512], f32))

        def sem(name):
            return ctx.enter_context(nc.semaphore(name))

        wa_raw = sb("wa_raw", [P, 3 * D])
        w12_raw = sb("w12_raw", [P, 2 * HID])
        h1_raw, h2_raw = sb("h1_raw", [P, KT, HID]), sb("h2_raw", [P, KT, HID])
        w3_raw = sb("w3_raw", [P, KT * D])
        sc = sb("sc", [P, N_SCALES])
        qk = sb("qk", [P, D])
        qk_hi, qk_lo = sb("qk_hi", [P, D], f32r), sb("qk_lo", [P, D], f32r)
        wv_hi, wv_lo = sb("wv_hi", [P, D], f32r), sb("wv_lo", [P, D], f32r)
        w12_hi, w12_lo = sb("w12_hi", [P, 2 * HID], f32r), sb("w12_lo", [P, 2 * HID], f32r)
        h1_hi, h1_lo = sb("h1_hi", [P, KT, HID], f32r), sb("h1_lo", [P, KT, HID], f32r)
        h2_hi, h2_lo = sb("h2_hi", [P, KT, HID], f32r), sb("h2_lo", [P, KT, HID], f32r)
        w3_hi, w3_lo = sb("w3_hi", [P, KT * D], f32r), sb("w3_lo", [P, KT * D], f32r)
        ident = sb("ident", [P, P])
        minus_half = sb("minus_half", [P, TB])
        ones = sb("ones", [P, 1])
        lo_abs = sb("lo_abs", [P, KT * HID])
        lo_sums = sb("lo_sums", [P, 4])
        flags = sb("flags", [1, 4])
        W12, H1, H2, W3 = range(4)

        xs = sb("xs", [P, TILES, D])
        x1 = sb("x1", [P, TILES, D])
        outs = sb("outs", [P, TILES, D])
        xn = sb("xn", [P, TB, D])
        xn2 = sb("xn2", [P, TB, D])
        probs = sb("probs", [P, TB, SEQ])
        y_n = sb("y_n", [P, TB, D])
        v_hi, v_lo = sb("v_hi", [P, TB, D], f32r), sb("v_lo", [P, TB, D], f32r)
        stats = sb("stats", [P, 4, TB, 6])
        mv = sb("mv", [P, 4, TB, 2])
        ve = sb("ve", [P, 4, TB])
        rstd = sb("rstd", [P, 4, TB])
        neg_max = sb("neg_max", [P, TB])
        sums = sb("sums", [P, TB])
        eps_s2 = sb("eps_s2", [P, TB])
        o_shift = sb("o_shift", [P, TILES])
        y_shift = sb("y_shift", [P, TB])
        LN_X, LN_O, LN_X1, LN_Y = range(4)

        xT_hi, xT_lo = sb("xT_hi", [P, TOK], f32r), sb("xT_lo", [P, TOK], f32r)
        gT_hi, gT_lo = sb("gT_hi", [P, TOK], f32r), sb("gT_lo", [P, TOK], f32r)
        pT_hi, pT_lo = sb("pT_hi", [P, 2, TOK], f32r), sb("pT_lo", [P, 2, TOK], f32r)
        x2T_hi, x2T_lo = sb("x2T_hi", [P, TOK], f32r), sb("x2T_lo", [P, TOK], f32r)
        silu1 = sb("silu1", [P, 2, TOK])
        act_full = sb("act_full", [P, 4, TOK])
        a1_hi, a1_lo = sb("a1_hi", [P, KT, TOK], f32r), sb("a1_lo", [P, KT, TOK], f32r)
        a2_hi, a2_lo = sb("a2_hi", [P, KT, TOK], f32r), sb("a2_lo", [P, KT, TOK], f32r)
        a3_hi, a3_lo = sb("a3_hi", [P, KT, TOK], f32r), sb("a3_lo", [P, KT, TOK], f32r)
        yT = sb("yT", [P, TOK])

        F = [bank(f"F{i}") for i in range(4)]
        A = [bank(f"A{i}") for i in range(4)]

        x_loaded = [sem(f"x_loaded{b}") for b in range(BLOCKS)]
        wa_loaded, w12_loaded, sc_loaded = sem("wa_loaded"), sem("w12_loaded"), sem("sc_loaded")
        h1_loaded, h2_loaded, w3_loaded = sem("h1_loaded"), sem("h2_loaded"), sem("w3_loaded")
        zeroed, ident_ready = sem("zeroed"), sem("ident_ready")
        qk_summed, qk_copied, qk_split, qk_ready = sem("qk_summed"), sem("qk_copied"), sem("qk_split"), sem("qk_ready")
        wv_split, wv_ready = sem("wv_split"), sem("wv_ready")
        w12_split, w12_ready = sem("w12_split"), sem("w12_ready")
        h1_split, h1_ready = sem("h1_split"), sem("h1_ready")
        h2_split, h2_ready = sem("h2_split"), sem("h2_ready")
        w3_split, w3_ready = sem("w3_split"), sem("w3_ready")
        lo_sums_ready, flags_in_psum, flags_ready = sem("lo_sums_ready"), sem("flags_in_psum"), sem("flags_ready")
        chain = sem("vector_chain")
        var_ready = [sem(f"var_ready{i}") for i in range(4)]
        rstd_ready = [sem(f"rstd_ready{i}") for i in range(4)]
        xn_ready, xT_in_psum, xT_hi_ready, xT_ready = sem("xn_ready"), sem("xT_in_psum"), sem("xT_hi_ready"), sem("xT_ready")
        gT_in_psum, gT_hi_ready, gT_ready = sem("gT_in_psum"), sem("gT_hi_ready"), sem("gT_ready")
        v_in_psum, v_hi_ready, v_ready = sem("v_in_psum"), sem("v_hi_ready"), sem("v_ready")
        scores_ready, max_ready, probs_ready, sums_ready = sem("scores_ready"), sem("max_ready"), sem("probs_ready"), sem("sums_ready")
        pT_in_psum, pT_hi_ready, pT_ready = sem("pT_in_psum"), sem("pT_hi_ready"), sem("pT_ready")
        o_in_psum, x1_ready, xn2_ready = sem("o_in_psum"), sem("x1_ready"), sem("xn2_ready")
        x2T_in_psum, x2T_hi_ready, x2T_ready = sem("x2T_in_psum"), sem("x2T_hi_ready"), sem("x2T_ready")
        up_in_psum, silu_ready, a1_full, a1_hi_ready, a1_ready = sem("up_in_psum"), sem("silu_ready"), sem("a1_full"), sem("a1_hi_ready"), sem("a1_ready")
        h1_in_psum, a2_full, a2_hi_ready, a2_lo_pool, a2_lo_dve = (
            sem("h1_in_psum"), sem("a2_full"), sem("a2_hi_ready"), sem("a2_lo_pool"), sem("a2_lo_dve"))
        h2_in_psum, a3_full, a3_hi_ready, a3_lo_pool, a3_lo_dve = (
            sem("h2_in_psum"), sem("a3_full"), sem("a3_hi_ready"), sem("a3_lo_pool"), sem("a3_lo_dve"))
        yT_in_psum, yT_ready, y_in_psum = sem("yT_in_psum"), sem("yT_ready"), sem("y_in_psum")
        y_shift_ready, yn_ready, out_ready, out_stored = sem("y_shift_ready"), sem("yn_ready"), sem("out_ready"), sem("out_stored")

        block = ctx.enter_context(nc.Block())

        @block.sync
        def _(sp):
            def load_x(b):
                sp.dma_start(xs[:, TB * b:TB * (b + 1), :].rearrange("p (g j) d -> p g (j d)", j=2),
                             x_view[:, 2 * b:2 * b + 2, :]).then_inc(x_loaded[b], 16)

            load_x(0)
            sp.dma_start(wa_raw[:, :], w_attn).then_inc(wa_loaded, 16)
            load_x(1)
            sp.dma_start(w12_raw[:, :], w12).then_inc(w12_loaded, 16)
            sp.dma_start(sc[:, :], scales).then_inc(sc_loaded, 16)
            sp.dma_start(h1_raw[:, :, :], h1.rearrange("(k p) o -> p k o", p=P)).then_inc(h1_loaded, 16)
            load_x(2)
            sp.dma_start(h2_raw[:, :, :], h2.rearrange("(k p) o -> p k o", p=P)).then_inc(h2_loaded, 16)
            load_x(3)
            sp.dma_start(w3_raw[:, :], w3).then_inc(w3_loaded, 16)
            for b in range(BLOCKS):
                sp.wait_ge(out_ready, b + 1)
                sp.dma_start(out_view[:, 2 * b:2 * b + 2, :],
                             outs[:, TB * b:TB * (b + 1), :].rearrange("p (g j) d -> p g (j d)", j=2)).then_inc(out_stored, 16)
            sp.wait_ge(out_stored, 16 * BLOCKS)

        @block.gpsimd
        def _(pool):
            nc.gpsimd.memset(ident[:, :], 0.0).then_inc(zeroed, 1)
            nc.gpsimd.memset(minus_half[:, :], -0.5).then_inc(zeroed, 1)
            nc.gpsimd.memset(ones[:, :], 1.0).then_inc(zeroed, 1)
            pool.wait_ge(zeroed, 3)
            nc.gpsimd.affine_select(out=ident[:, :], in_=ident[:, :], compare_op=ALU.not_equal, fill=1.0, base=0,
                                    pattern=[[-1, P]], channel_multiplier=1).then_inc(ident_ready, 1)

            def rsqrt(ln, b):
                pool.wait_ge(var_ready[ln], b + 1)
                nc.gpsimd.tensor_tensor(rstd[:, ln, :], ve[:, ln, :], minus_half[:, :], ALU.pow).then_inc(rstd_ready[ln], 1)

            def lo_part(b, o, dst, hi, hi_sem, full_sem, done):
                pool.wait_ge(hi_sem, KT * b + o + 1)
                pool.wait_ge(full_sem, KT * b + o + 1)
                nc.gpsimd.tensor_tensor(dst[:, o, :], act_full[:, o, :], hi[:, o, :].bitcast(f32), ALU.subtract).then_inc(done, 1)

            def last_add(b):
                pool.wait_ge(yn_ready, TB * (b + 1))
                pool.wait_ge(x1_ready, b + 1)
                nc.gpsimd.tensor_tensor(outs[:, TB * b:TB * (b + 1), :], y_n[:, :, :],
                                        x1[:, TB * b:TB * (b + 1), :], ALU.add).then_inc(out_ready, 1)

            rsqrt(LN_X, 0)
            rsqrt(LN_X, 1)
            rsqrt(LN_O, 0)
            rsqrt(LN_X1, 0)
            for b in range(BLOCKS):
                if b > 0:
                    rsqrt(LN_Y, b - 1)
                if b + 2 < BLOCKS:
                    rsqrt(LN_X, b + 2)
                lo_part(b, 0, a2_lo, a2_hi, a2_hi_ready, a2_full, a2_lo_pool)
                if b > 0:
                    last_add(b - 1)
                lo_part(b, 1, a2_lo, a2_hi, a2_hi_ready, a2_full, a2_lo_pool)
                if b + 1 < BLOCKS:
                    rsqrt(LN_O, b + 1)
                    rsqrt(LN_X1, b + 1)
                lo_part(b, 0, a3_lo, a3_hi, a3_hi_ready, a3_full, a3_lo_pool)
                lo_part(b, 1, a3_lo, a3_hi, a3_hi_ready, a3_full, a3_lo_pool)
            rsqrt(LN_Y, BLOCKS - 1)
            last_add(BLOCKS - 1)

        @block.scalar
        def _(act):
            def hi_from_psum(dst, src, ready, n, done):
                act.wait_ge(ready, n)
                nc.scalar.activation(dst, src, ACT.Copy).then_inc(done, 1)

            def exps(b):
                for t in range(TB):
                    g, j = divmod(t, 2)
                    if j == 0:
                        act.wait_ge(max_ready, 2 * b + g + 1)
                    if b > 0 and t == 0:
                        act.wait_ge(pT_in_psum, 2 * b)
                        act.wait_ge(x1_ready, b)
                    nc.scalar.activation(probs[:, t, :], S_BANK[g][:, j * SEQ:(j + 1) * SEQ], ACT.Exp,
                                         bias=neg_max[:, t:t + 1], accum_out=sums[:, t:t + 1]).then_inc(probs_ready, 1)

            def front(b, part):
                if part == 0:
                    if b > 0:
                        act.wait_ge(scores_ready, 2 * b)
                    hi_from_psum(xT_hi[:, :], A[0][:, :], xT_in_psum, b + 1, xT_hi_ready)
                else:
                    hi_from_psum(gT_hi[:, :], A[1][:, :], gT_in_psum, b + 1, gT_hi_ready)
                    if b > 0:
                        act.wait_ge(o_in_psum, b)
                    hi_from_psum(v_hi[:, :, :], A[2][:, :], v_in_psum, b + 1, v_hi_ready)

            def probs_hi(b):
                for g in range(2):
                    if b > 0 and g == 0:
                        act.wait_ge(o_in_psum, b)
                    hi_from_psum(pT_hi[:, g, :], PT_BANK[g][:, :], pT_in_psum, 2 * b + g + 1, pT_hi_ready)

            def x2T(b):
                if b > 0:
                    act.wait_ge(up_in_psum, KT * b)
                hi_from_psum(x2T_hi[:, :], A[3][:, :], x2T_in_psum, b + 1, x2T_hi_ready)

            def silus(b):
                for o in range(KT):
                    act.wait_ge(up_in_psum, KT * b + o + 1)
                    if KT * b + o >= 2:
                        act.wait_ge(a1_full, KT * b + o - 1)
                    nc.scalar.activation(silu1[:, o % 2, :], F[2 * (o % 2)][:, :], ACT.Silu,
                                         scale=sc[:, S_W1 + o:S_W1 + o + 1]).then_inc(silu_ready, 1)

            def gelu(b, o, first_scale, in_psum, used_sem, used, free_sem, hi, hi_done, full_done):
                act.wait_ge(in_psum, KT * b + o + 1)
                scale = sc[:, first_scale + o:first_scale + o + 1]
                if b > 0 and o == 0:
                    act.wait_ge(used_sem, used)
                nc.scalar.activation(hi[:, o, :], F[o][:, :], ACT.Gelu, scale=scale).then_inc(hi_done, 1)
                act.wait_ge(*free_sem)
                nc.scalar.activation(act_full[:, o, :], F[o][:, :], ACT.Gelu, scale=scale).then_inc(full_done, 1)

            def gelu1(b, o):
                gelu(b, o, S_H1, h1_in_psum, h2_in_psum, KT * b, (a1_ready, KT * b + o + 1), a2_hi, a2_hi_ready, a2_full)

            def gelu2(b, o):
                free = (a2_lo_pool, 2 * b + o + 1) if o < 2 else (a2_lo_dve, 2 * b + o - 1)
                gelu(b, o, S_H2, h2_in_psum, yT_in_psum, b, free, a3_hi, a3_hi_ready, a3_full)

            def scaled_yT(b):
                act.wait_ge(yT_in_psum, b + 1)
                if b > 0:
                    act.wait_ge(y_in_psum, b)
                nc.scalar.activation(yT[:, :], A[1][:, :], ACT.Copy, scale=sc[:, S_W3:S_W3 + 1]).then_inc(yT_ready, 1)

            def y_normalised(b):
                act.wait_ge(y_shift_ready, b + 1)
                if b > 0:
                    act.wait_ge(out_ready, b)
                for t in range(TB):
                    nc.scalar.activation(y_n[:, t, :], A[2][:, t * D:(t + 1) * D], ACT.Identity,
                                         bias=y_shift[:, t:t + 1], scale=rstd[:, LN_Y, t:t + 1]).then_inc(yn_ready, 1)

            def weights_hi(dst, raw, loaded, split):
                act.wait_ge(loaded, 16)
                nc.scalar.activation(dst, raw, ACT.Copy).then_inc(split, 1)

            def sum_of_lo(n, lo, ready, count):
                act.wait_ge(ready, count)
                if n > 0:
                    act.wait_ge(lo_sums_ready, n)
                nc.scalar.activation(lo_abs[:, 0:LO_COLUMNS[n]], lo, ACT.Abs,
                                     accum_out=lo_sums[:, n:n + 1]).then_inc(lo_sums_ready, 1)

            LO_COLUMNS = (2 * HID, KT * HID, KT * HID, KT * D)
            S_BANK = (A[3], A[0])
            PT_BANK = (A[3], A[1])

            act.wait_ge(qk_summed, 1)
            nc.scalar.activation(qk[:, :], F[0][:, 0:D], ACT.Copy, scale=SCALE).then_inc(qk_copied, 1)
            act.wait_ge(sc_loaded, 16)
            front(0, 0)
            weights_hi(w12_hi[:, :], w12_raw[:, :], w12_loaded, w12_split)
            front(0, 1)
            exps(0)
            for k in range(KT):
                weights_hi(h1_hi[:, k, :], h1_raw[:, k, :], h1_loaded, h1_split)
            probs_hi(0)
            sum_of_lo(W12, w12_lo[:, :], w12_ready, 1)
            x2T(0)
            front(1, 0)
            for k in range(KT):
                weights_hi(h2_hi[:, k, :], h2_raw[:, k, :], h2_loaded, h2_split)
            front(1, 1)
            sum_of_lo(H1, h1_lo[:, :, :].rearrange("p k o -> p (k o)"), h1_ready, KT)
            weights_hi(w3_hi[:, :], w3_raw[:, :], w3_loaded, w3_split)
            silus(0)
            for b in range(BLOCKS):
                if b + 1 < BLOCKS:
                    exps(b + 1)
                    probs_hi(b + 1)
                if b == 0:
                    sum_of_lo(H2, h2_lo[:, :, :].rearrange("p k o -> p (k o)"), h2_ready, KT)
                    sum_of_lo(W3, w3_lo[:, :], w3_ready, 1)
                else:
                    y_normalised(b - 1)
                for o in range(KT):
                    gelu1(b, o)
                gelu2(b, 0)
                if b + 2 < BLOCKS:
                    front(b + 2, 0)
                gelu2(b, 1)
                gelu2(b, 2)
                if b + 1 < BLOCKS:
                    x2T(b + 1)
                if b + 2 < BLOCKS:
                    front(b + 2, 1)
                gelu2(b, 3)
                if b + 1 < BLOCKS:
                    silus(b + 1)
                scaled_yT(b)
            y_normalised(BLOCKS - 1)

        @block.vector
        def _(dve):
            links = [0]

            def link(ins):
                links[0] += 1
                ins.then_inc(chain, 1)
                dve.wait_ge(chain, links[0])

            def lo_part(dst, full, hi, hi_sem, n, done):
                dve.wait_ge(hi_sem, n)
                nc.vector.tensor_tensor(dst, full, hi.bitcast(f32), ALU.subtract).then_inc(done, 1)

            def statistics(ln, tiles):
                for t in range(TB):
                    last = nc.vector.bn_stats(stats[:, ln, t, :], tiles(t))
                link(last)
                for t in range(TB):
                    last = nc.vector.bn_aggr(mv[:, ln, t, :], stats[:, ln, t, :])
                link(last)

            def x_norm(b):
                if b > 0:
                    dve.wait_ge(xT_in_psum, b)
                dve.wait_ge(x_loaded[b], 16)
                statistics(LN_X, lambda t: xs[:, TB * b + t, :])
                nc.vector.tensor_scalar(ve[:, LN_X, :], mv[:, LN_X, :, 1], EPS, None, ALU.add).then_inc(var_ready[LN_X], 1)
                normalise(b, LN_X, lambda t: xs[:, TB * b + t, :], xn, xn_ready)

            def normalise(b, ln, src, dst, done):
                dve.wait_ge(rstd_ready[ln], b + 1)
                for t in range(TB):
                    nc.vector.tensor_scalar(dst[:, t, :], src(t), mv[:, ln, t, 0:1], rstd[:, ln, t:t + 1],
                                            ALU.subtract, ALU.mult).then_inc(done, 1)

            def maxima(b):
                for g, s in enumerate((A[3], A[0])):
                    dve.wait_ge(scores_ready, 2 * b + g + 1)
                    if b > 0 and g == 0:
                        dve.wait_ge(probs_ready, TB * b)
                    nc.vector.tensor_reduce(neg_max[:, 2 * g:2 * g + 2], s[:, :].rearrange("p (j m) -> p j m", j=2),
                                            AX, ALU.max, negate=True).then_inc(max_ready, 1)

            def xT_part(b):
                lo_part(xT_lo[:, :], A[0][:, :], xT_hi[:, :], xT_hi_ready, b + 1, xT_ready)

            def gv_part(b):
                lo_part(gT_lo[:, :], A[1][:, :], gT_hi[:, :], gT_hi_ready, b + 1, gT_ready)
                lo_part(v_lo[:, :, :], A[2][:, :].rearrange("p (t d) -> p t d", t=TB), v_hi[:, :, :], v_hi_ready, b + 1, v_ready)

            def probs_lo(b):
                dve.wait_ge(probs_ready, TB * (b + 1))
                nc.vector.scalar_tensor_tensor(eps_s2[:, :], sums[:, :], EPS, sums[:, :], ALU.mult, ALU.mult).then_inc(sums_ready, 1)
                for g, s in enumerate((A[3], A[1])):
                    lo_part(pT_lo[:, g, :], s[:, :], pT_hi[:, g, :], pT_hi_ready, 2 * b + g + 1, pT_ready)

            def attention_out(b):
                dve.wait_ge(o_in_psum, b + 1)
                o = lambda t: A[2][:, t * D:(t + 1) * D]
                statistics(LN_O, o)
                dve.wait_ge(sums_ready, b + 1)
                nc.vector.tensor_tensor(ve[:, LN_O, :], mv[:, LN_O, :, 1], eps_s2[:, :], ALU.add).then_inc(var_ready[LN_O], 1)
                dve.wait_ge(rstd_ready[LN_O], b + 1)
                for t in range(TB):
                    last = nc.vector.scalar_tensor_tensor(x1[:, TB * b + t, :], o(t), rstd[:, LN_O, t:t + 1], xs[:, TB * b + t, :],
                                                          ALU.mult, ALU.add)
                last.then_inc(x1_ready, 1)
                nc.vector.tensor_tensor(o_shift[:, TB * b:TB * (b + 1)], mv[:, LN_O, :, 0], rstd[:, LN_O, :], ALU.mult)
                dve.wait_ge(x1_ready, b + 1)
                x1t = lambda t: x1[:, TB * b + t, :]
                statistics(LN_X1, x1t)
                nc.vector.tensor_scalar(ve[:, LN_X1, :], mv[:, LN_X1, :, 1], EPS, None, ALU.add).then_inc(var_ready[LN_X1], 1)
                if b > 0:
                    dve.wait_ge(x2T_in_psum, b)
                normalise(b, LN_X1, x1t, xn2, xn2_ready)

            def x2T_part(b):
                lo_part(x2T_lo[:, :], A[3][:, :], x2T_hi[:, :], x2T_hi_ready, b + 1, x2T_ready)

            def gated(b, o):
                dve.wait_ge(silu_ready, KT * b + o + 1)
                if b > 0 and o < 2:
                    dve.wait_ge(a3_lo_pool, 2 * (b - 1) + o + 1)
                elif b > 0:
                    dve.wait_ge(a3_lo_dve, 2 * (b - 1) + o - 1)
                nc.vector.scalar_tensor_tensor(act_full[:, o, :], F[2 * (o % 2) + 1][:, :], sc[:, S_W2 + o:S_W2 + o + 1],
                                               silu1[:, o % 2, :], ALU.mult, ALU.mult).then_inc(a1_full, 1)
                if b > 0 and o == 0:
                    dve.wait_ge(h1_in_psum, KT * b)
                dve.wait_ge(a1_full, KT * b + o + 1)
                nc.vector.tensor_copy(a1_hi[:, o, :], act_full[:, o, :]).then_inc(a1_hi_ready, 1)

            HALF = KT // 2

            def act_lo(b, o, dst, hi, hi_sem, full_sem, done):
                dve.wait_ge(full_sem, KT * b + o + 1)
                lo_part(dst[:, o, :], act_full[:, o, :], hi[:, o, :], hi_sem, KT * b + o + 1, done)

            def gates(b):
                gated(b, 0)
                for o in range(1, KT):
                    gated(b, o)
                    act_lo(b, o - 1, a1_lo, a1_hi, a1_hi_ready, a1_full, a1_ready)
                act_lo(b, KT - 1, a1_lo, a1_hi, a1_hi_ready, a1_full, a1_ready)

            def y_norm(b):
                dve.wait_ge(y_in_psum, b + 1)
                if b > 0:
                    dve.wait_ge(yn_ready, TB * b)
                statistics(LN_Y, lambda t: A[2][:, t * D:(t + 1) * D])
                nc.vector.tensor_scalar(ve[:, LN_Y, :], mv[:, LN_Y, :, 1], EPS, None, ALU.add).then_inc(var_ready[LN_Y], 1)
                dve.wait_ge(rstd_ready[LN_Y], b + 1)
                link(nc.vector.tensor_tensor(y_shift[:, :], mv[:, LN_Y, :, 0], rstd[:, LN_Y, :], ALU.mult))
                nc.vector.scalar_tensor_tensor(y_shift[:, :], y_shift[:, :], -1.0, o_shift[:, TB * b:TB * (b + 1)],
                                               ALU.mult, ALU.subtract).then_inc(y_shift_ready, 1)

            def copy_flags(half, source):
                dve.wait_ge(flags_in_psum, half + 1)
                c = slice(2 * half, 2 * half + 2)
                nc.vector.tensor_copy(flags[0:1, c], source[0:1, c]).then_inc(flags_ready, 1)

            dve.wait_ge(wa_loaded, 16)
            nc.vector.tensor_copy(wv_hi[:, :], wa_raw[:, 2 * D:3 * D]).then_inc(wv_split, 1)
            lo_part(wv_lo[:, :], wa_raw[:, 2 * D:3 * D], wv_hi[:, :], wv_split, 1, wv_ready)
            x_norm(0)
            dve.wait_ge(qk_copied, 1)
            nc.vector.tensor_copy(qk_hi[:, :], qk[:, :]).then_inc(qk_split, 1)
            lo_part(qk_lo[:, :], qk[:, :], qk_hi[:, :], qk_split, 1, qk_ready)
            xT_part(0)
            gv_part(0)
            maxima(0)
            x_norm(1)
            lo_part(w12_lo[:, :], w12_raw[:, :], w12_hi[:, :], w12_split, 1, w12_ready)
            probs_lo(0)
            for k in range(KT):
                lo_part(h1_lo[:, k, :], h1_raw[:, k, :], h1_hi[:, k, :], h1_split, k + 1, h1_ready)
            attention_out(0)
            x2T_part(0)
            xT_part(1)
            gv_part(1)
            for k in range(KT):
                lo_part(h2_lo[:, k, :], h2_raw[:, k, :], h2_hi[:, k, :], h2_split, k + 1, h2_ready)
            maxima(1)
            copy_flags(0, F[0])
            gates(0)
            lo_part(w3_lo[:, :], w3_raw[:, :], w3_hi[:, :], w3_split, 1, w3_ready)
            for b in range(BLOCKS):
                if b + 1 < BLOCKS:
                    probs_lo(b + 1)
                if b > 0:
                    y_norm(b - 1)
                if b + 2 < BLOCKS:
                    x_norm(b + 2)
                act_lo(b, 2, a2_lo, a2_hi, a2_hi_ready, a2_full, a2_lo_dve)
                if b == 0:
                    copy_flags(1, A[2])
                act_lo(b, 3, a2_lo, a2_hi, a2_hi_ready, a2_full, a2_lo_dve)
                if b + 1 < BLOCKS:
                    attention_out(b + 1)
                if b + 2 < BLOCKS:
                    xT_part(b + 2)
                act_lo(b, 2, a3_lo, a3_hi, a3_hi_ready, a3_full, a3_lo_dve)
                if b + 1 < BLOCKS:
                    x2T_part(b + 1)
                if b + 2 < BLOCKS:
                    gv_part(b + 2)
                act_lo(b, 3, a3_lo, a3_hi, a3_hi_ready, a3_full, a3_lo_dve)
                if b + 2 < BLOCKS:
                    maxima(b + 2)
                if b + 1 < BLOCKS:
                    gates(b + 1)
            y_norm(BLOCKS - 1)

        @block.tensor
        def _(pe):
            def product(out, terms):
                last = None
                for n, (w_hi, w_lo, x_hi, x_lo) in enumerate(terms):
                    for m, (w, v) in enumerate(((w_hi, x_hi), (w_hi, x_lo), (w_lo, x_hi))):
                        last = nc.tensor.matmul(out, w, v, start=(n == 0 and m == 0), stop=(n == len(terms) - 1 and m == 2))
                return last

            def ffn_hi(out, terms):
                for n, (w_hi, _, x_hi, _) in enumerate(terms):
                    nc.tensor.matmul(out, w_hi, x_hi, start=(n == 0), stop=False)

            def ffn_w_lo(flag, products):
                with pe.If(flag != 0):
                    for out, terms in products:
                        for _, w_lo, x_hi, _ in terms:
                            nc.tensor.matmul(out, w_lo, x_hi, start=False, stop=False)

            def ffn_lo(out, terms):
                for n, (w_hi, _, _, x_lo) in enumerate(terms):
                    last = nc.tensor.matmul(out, w_hi, x_lo, start=False, stop=(n == len(terms) - 1))
                return last

            def sum_flags(half, out):
                pe.wait_ge(lo_sums_ready, 2 * half + 2)
                c = slice(2 * half, 2 * half + 2)
                nc.tensor.matmul(out[0:1, c], ones[:, :], lo_sums[:, c], start=True, stop=True).then_inc(flags_in_psum, 1)

            def read_flag(n):
                pe.wait_ge(flags_ready, n // 2 + 1)
                flag[n] = pe.value_load(flags[0:1, n:n + 1].bitcast(mybir.dt.int32))

            flag = {}

            def front_transposes(b):
                pe.wait_ge(xn_ready, TB * (b + 1))
                if b > 0:
                    pe.wait_ge(probs_ready, TB * b)
                for t in range(TB):
                    last = nc.tensor.transpose(A[0][:, t * P:(t + 1) * P], xn[:, t, :], ident[:, :])
                last.then_inc(xT_in_psum, 1)

            def front_projections(b):
                pe.wait_ge(xT_ready, b + 1)
                if b > 0:
                    pe.wait_ge(pT_ready, 2 * b)
                else:
                    pe.wait_ge(qk_ready, 1)
                    pe.wait_ge(wv_ready, 1)
                product(A[1][:, :], [(qk_hi[:, :], qk_lo[:, :], xT_hi[:, :], xT_lo[:, :])]).then_inc(gT_in_psum, 1)
                if b > 0:
                    pe.wait_ge(x1_ready, b)
                for t in range(TB):
                    c = slice(t * P, (t + 1) * P)
                    last = product(A[2][:, c], [(xT_hi[:, c], xT_lo[:, c], wv_hi[:, :], wv_lo[:, :])])
                last.then_inc(v_in_psum, 1)

            def front_scores(b):
                pe.wait_ge(gT_ready, b + 1)
                if b > 0:
                    pe.wait_ge(x2T_ready, b)
                for g, s in enumerate((A[3], A[0])):
                    keys = slice(g * SEQ, (g + 1) * SEQ)
                    for j in range(2):
                        c = slice((2 * g + j) * P, (2 * g + j + 1) * P)
                        last = product(s[:, j * SEQ:(j + 1) * SEQ], [(gT_hi[:, c], gT_lo[:, c], xT_hi[:, keys], xT_lo[:, keys])])
                    last.then_inc(scores_ready, 1)

            def probs_transposes(b):
                for g, s in enumerate((A[3], A[1])):
                    pe.wait_ge(probs_ready, TB * b + 2 * g + 2)
                    if g == 0:
                        pe.wait_ge(ident_ready, 1)
                    elif b >= 2:
                        pe.wait_ge(yT_ready, b - 1)
                    elif b == 0:
                        pe.wait_ge(gT_ready, 1)
                    for h in range(2):
                        for j in range(2):
                            c = (2 * h + j) * P
                            last = nc.tensor.transpose(s[:, c:c + P], probs[:, 2 * g + j, h * P:(h + 1) * P], ident[:, :])
                    last.then_inc(pT_in_psum, 1)

            def attend(b):
                pe.wait_ge(v_ready, b + 1)
                if b >= 2:
                    pe.wait_ge(yn_ready, TB * (b - 1))
                for t in range(TB):
                    g, j = divmod(t, 2)
                    if j == 0:
                        pe.wait_ge(pT_ready, 2 * b + g + 1)
                    last = product(A[2][:, t * D:(t + 1) * D],
                                   [(pT_hi[:, g, (2 * h + j) * P:(2 * h + j + 1) * P], pT_lo[:, g, (2 * h + j) * P:(2 * h + j + 1) * P],
                                     v_hi[:, 2 * g + h, :], v_lo[:, 2 * g + h, :]) for h in range(2)])
                last.then_inc(o_in_psum, 1)

            def x2_transposes(b):
                pe.wait_ge(pT_ready, 2 * b + 1)
                pe.wait_ge(xn2_ready, TB * (b + 1))
                for t in range(TB):
                    last = nc.tensor.transpose(A[3][:, t * P:(t + 1) * P], xn2[:, t, :], ident[:, :])
                last.then_inc(x2T_in_psum, 1)

            def ffn_product(n, groups, lo_sems, lo_n):
                for out, terms in groups:
                    ffn_hi(out, terms)
                ffn_w_lo(flag[n], groups)
                for sem_, n_ in zip(lo_sems, lo_n):
                    pe.wait_ge(sem_, n_)
                return [ffn_lo(out, terms) for out, terms in groups]

            def up(b):
                pe.wait_ge(x2T_ready, b + 1)
                for o in range(KT):
                    if o >= 2:
                        pe.wait_ge(a1_full, KT * b + o - 1)
                    elif b > 0:
                        pe.wait_ge(a3_full, KT * (b - 1) + 2 * o + 2)
                    columns = [slice(m * HID + o * P, m * HID + (o + 1) * P) for m in range(2)]
                    ffn_product(W12, [(F[2 * (o % 2) + m][:, :], [(w12_hi[:, c], w12_lo[:, c], x2T_hi[:, :], x2T_lo[:, :])])
                                      for m, c in enumerate(columns)], [], [])[-1].then_inc(up_in_psum, 1)

            def hidden(b, slices, flag_n, w_hi, w_lo, x_hi, x_lo, bank_free, hi_wait, lo_waits, done):
                for o in slices:
                    pe.wait_ge(bank_free[0], bank_free[1](o))
                    if o == 0:
                        pe.wait_ge(*hi_wait)
                groups = []
                for o in slices:
                    c = slice(o * P, (o + 1) * P)
                    groups.append((F[o][:, :], [(w_hi[:, k, c], w_lo[:, k, c], x_hi[:, k, :], x_lo[:, k, :]) for k in range(KT)]))
                first = slices[0] == 0
                for last in ffn_product(flag_n, groups, [w[0] for w in lo_waits] if first else [], [w[1] for w in lo_waits] if first else []):
                    last.then_inc(done, 1)

            def down(b):
                pe.wait_ge(a3_hi_ready, KT * (b + 1))
                pe.wait_ge(gT_ready, min(b + 3, BLOCKS))
                ffn_product(W3, [(A[1][:, :], [(w3_hi[:, k * D:(k + 1) * D], w3_lo[:, k * D:(k + 1) * D], a3_hi[:, k, :], a3_lo[:, k, :])
                                               for k in range(KT)])],
                            [a3_lo_pool, a3_lo_dve], [2 * (b + 1), 2 * (b + 1)])[0].then_inc(yT_in_psum, 1)

            def y_transposes(b):
                pe.wait_ge(yT_ready, b + 1)
                pe.wait_ge(v_ready, min(b + 3, BLOCKS))
                for t in range(TB):
                    last = nc.tensor.transpose(A[2][:, t * P:(t + 1) * P], yT[:, t * P:(t + 1) * P], ident[:, :])
                last.then_inc(y_in_psum, 1)

            def h1_layer(b, slices):
                hidden(b, slices, H1, h1_hi, h1_lo, a1_hi, a1_lo, (a1_full, lambda o: KT * b + 3 + o // 2),
                       (a1_hi_ready, KT * (b + 1)), [(a1_ready, KT * (b + 1))], h1_in_psum)

            def h2_layer(b, slices):
                hidden(b, slices, H2, h2_hi, h2_lo, a2_hi, a2_lo, (a2_full, lambda o: KT * b + o + 1),
                       (a2_hi_ready, KT * (b + 1)), [(a2_lo_pool, 2 * (b + 1)), (a2_lo_dve, 2 * (b + 1))], h2_in_psum)

            pe.wait_ge(wa_loaded, 16)
            nc.tensor.matmul(F[0][:, 0:D], wa_raw[:, 0:D], wa_raw[:, D:2 * D], start=True, stop=True).then_inc(qk_summed, 1)
            pe.wait_ge(ident_ready, 1)
            front_transposes(0)
            front_projections(0)
            front_scores(0)
            probs_transposes(0)
            attend(0)
            x2_transposes(0)
            front_transposes(1)
            front_projections(1)
            front_scores(1)
            pe.wait_ge(qk_copied, 1)
            sum_flags(0, F[0])
            read_flag(W12)
            read_flag(H1)
            up(0)
            for b in range(BLOCKS):
                if b > 0:
                    y_transposes(b - 1)
                if b + 1 < BLOCKS:
                    probs_transposes(b + 1)
                h1_layer(b, (0, 1))
                if b == 0:
                    pe.wait_ge(v_ready, 2)
                    sum_flags(1, A[2])
                h1_layer(b, (2,))
                h1_layer(b, (3,))
                if b == 0:
                    read_flag(H2)
                    read_flag(W3)
                if b + 1 < BLOCKS:
                    attend(b + 1)
                h2_layer(b, (0, 1))
                if b + 2 < BLOCKS:
                    front_transposes(b + 2)
                h2_layer(b, (2,))
                if b + 1 < BLOCKS:
                    x2_transposes(b + 1)
                if b + 2 < BLOCKS:
                    front_projections(b + 2)
                h2_layer(b, (3,))
                if b + 2 < BLOCKS:
                    front_scores(b + 2)
                if b + 1 < BLOCKS:
                    up(b + 1)
                down(b)
            y_transposes(BLOCKS - 1)


def kernel(**inputs):
    import concourse.bacc as bacc
    from concourse.bass_utils import run_bass_kernel_spmd

    a = {name: np.asarray(value) for name, value in inputs.items()}
    w_qkv = a["L0_attn_W_qkv"]
    arrays = {
        "x": a["L0_attn_x"],
        "w_attn": np.concatenate([w_qkv[:D], w_qkv[D:2 * D], w_qkv[2 * D:].T], axis=1),
        "w12": np.concatenate([a["L0_ffn_w1_w"].T, a["L0_ffn_w2_w"].T], axis=1),
        "h1": a["L0_ffn_h1_w"].T,
        "h2": a["L0_ffn_h2_w"].T,
        "w3": a["L0_ffn_w3_w"].T.reshape(KT, P, D).transpose(1, 0, 2).reshape(P, KT * D),
        "scales": np.concatenate([a["L0_ffn_" + n].reshape(-1, P) for n in ("w1_s", "w2_s", "h1_s", "h2_s", "w3_s")]).T,
    }
    arrays = {name: np.ascontiguousarray(value) for name, value in arrays.items()}
    nc = bacc.Bacc("TRN2", target_bir_lowering=False, num_devices=1)
    args = [nc.dram_tensor(name, v.shape, mybir.dt.from_np(v.dtype), kind="ExternalInput").ap() for name, v in arrays.items()]
    out = nc.dram_tensor("out", (BATCHES, SEQ, D), mybir.dt.float32, kind="ExternalOutput").ap()
    sandwich_kernel(nc, *args, out)
    result = run_bass_kernel_spmd(nc, [arrays], core_ids=[0])
    return result.results[0]["out"]
```

```python
from contextlib import ExitStack

import numpy as np

import concourse.bass as bass
from concourse import mybir

P = 128
BATCHES, SEQ, D = 8, 256, 128
HID = 512
TILES = BATCHES * SEQ // P
TB = 4
TOK = TB * P
BLOCKS = TILES // TB
LAST = BLOCKS - 1
KT = HID // P
EPS = 1e-5
SCALE = float(D) ** -0.5

WARM = (8, 10, 6, 4, 4, 4, 12, 2)

S_W1, S_W2, S_H1, S_H2, S_W3 = 0, KT, 2 * KT, 3 * KT, 4 * KT
N_SCALES = 4 * KT + 1


def sandwich_kernel(nc, x, w_attn, w12, h1, h2, w3, scales, out):
    f32, f32r = mybir.dt.float32, mybir.dt.float32r
    ACT, ALU = mybir.ActivationFunctionType, mybir.AluOpType
    AX = mybir.AxisListType.X

    x_view = x.rearrange("g (p j) d -> p g (j d)", j=2)
    out_view = out.rearrange("g (p j) d -> p g (j d)", j=2)

    ctx = ExitStack()
    with ctx:
        def sb(name, shape, dt=f32):
            return ctx.enter_context(nc.sbuf_tensor(name, shape, dt))

        def bank(name):
            return ctx.enter_context(nc.psum_tensor(name, [P, 512], f32))

        def sem(name):
            return ctx.enter_context(nc.semaphore(name))

        wa_raw = sb("wa_raw", [P, 3 * D])
        w12_raw = sb("w12_raw", [P, 2 * HID])
        h1_raw, h2_raw = sb("h1_raw", [P, KT, HID]), sb("h2_raw", [P, KT, HID])
        w3_raw = sb("w3_raw", [P, KT * D])
        sc = sb("sc", [P, N_SCALES])
        qk = sb("qk", [P, D])
        qk_hi, qk_lo = sb("qk_hi", [P, D], f32r), sb("qk_lo", [P, D], f32r)
        wv_hi, wv_lo = sb("wv_hi", [P, D], f32r), sb("wv_lo", [P, D], f32r)
        w12_hi, w12_lo = sb("w12_hi", [P, 2 * HID], f32r), sb("w12_lo", [P, 2 * HID], f32r)
        h1_hi, h1_lo = sb("h1_hi", [P, KT, HID], f32r), sb("h1_lo", [P, KT, HID], f32r)
        h2_hi, h2_lo = sb("h2_hi", [P, KT, HID], f32r), sb("h2_lo", [P, KT, HID], f32r)
        w3_hi, w3_lo = sb("w3_hi", [P, KT * D], f32r), sb("w3_lo", [P, KT * D], f32r)
        ident = sb("ident", [P, P])
        minus_half = sb("minus_half", [P, TB])
        ones = sb("ones", [P, 1])
        warm = sb("warm", [P, 512], mybir.dt.bfloat16)
        lo_abs = sb("lo_abs", [P, KT * HID])
        lo_sums = sb("lo_sums", [P, 4])
        flags = sb("flags", [1, 4])
        W12, H1, H2, W3 = range(4)
        FLAG_GROUPS = ((W12, H1 + 1), (H2, W3 + 1))
        POOL_A1, POOL_A2, POOL_A3 = 3, 3, 3

        xs = sb("xs", [P, TILES, D])
        x1 = sb("x1", [P, TILES, D])
        outs = sb("outs", [P, TILES, D])
        xn = sb("xn", [P, TB, D])
        xn2 = sb("xn2", [P, TB, D])
        probs = sb("probs", [P, TB, SEQ])
        y_n = sb("y_n", [P, TB, D])
        v_hi, v_lo = sb("v_hi", [P, TB, D], f32r), sb("v_lo", [P, TB, D], f32r)
        stats = sb("stats", [P, 4, TB, 6])
        mv = sb("mv", [P, 4, TB, 2])
        ve = sb("ve", [P, 4, TB])
        rstd = sb("rstd", [P, 4, TB])
        neg_max = sb("neg_max", [P, TB])
        sums = sb("sums", [P, TB])
        eps_s2 = sb("eps_s2", [P, TB])
        o_shift = sb("o_shift", [P, TILES])
        y_shift = sb("y_shift", [P, TB])
        LN_X, LN_O, LN_X1, LN_Y = range(4)

        xT_hi, xT_lo = sb("xT_hi", [P, TOK], f32r), sb("xT_lo", [P, TOK], f32r)
        gT_hi, gT_lo = sb("gT_hi", [P, TOK], f32r), sb("gT_lo", [P, TOK], f32r)
        pT_hi, pT_lo = sb("pT_hi", [P, 2, TOK], f32r), sb("pT_lo", [P, 2, TOK], f32r)
        oT = sb("oT", [P, TOK])
        x2T_hi, x2T_lo = sb("x2T_hi", [P, TOK], f32r), sb("x2T_lo", [P, TOK], f32r)
        silu1 = sb("silu1", [P, 2, TOK])
        act_full = sb("act_full", [P, 4, TOK])
        a1_hi, a1_lo = sb("a1_hi", [P, KT, TOK], f32r), sb("a1_lo", [P, KT, TOK], f32r)
        a2_hi, a2_lo = sb("a2_hi", [P, KT, TOK], f32r), sb("a2_lo", [P, KT, TOK], f32r)
        a3_hi, a3_lo = sb("a3_hi", [P, KT, TOK], f32r), sb("a3_lo", [P, KT, TOK], f32r)
        yT = sb("yT", [P, TOK])

        F = [bank(f"F{i}") for i in range(4)]
        A = [bank(f"A{i}") for i in range(4)]

        x_loaded = [sem(f"x_loaded{b}") for b in range(BLOCKS)]
        wa_loaded, w12_loaded, sc_loaded = sem("wa_loaded"), sem("w12_loaded"), sem("sc_loaded")
        h1_loaded, h2_loaded, w3_loaded = sem("h1_loaded"), sem("h2_loaded"), sem("w3_loaded")
        warm_ready = sem("warm_ready")
        zeroed, ident_ready = sem("zeroed"), sem("ident_ready")
        qk_summed, qk_copied, qk_split, qk_ready = sem("qk_summed"), sem("qk_copied"), sem("qk_split"), sem("qk_ready")
        wv_split, wv_ready = sem("wv_split"), sem("wv_ready")
        w12_split, w12_ready = sem("w12_split"), sem("w12_ready")
        h1_split, h1_ready = sem("h1_split"), sem("h1_ready")
        h2_split, h2_ready = sem("h2_split"), sem("h2_ready")
        w3_split, w3_ready = sem("w3_split"), sem("w3_ready")
        lo_sums_ready, flags_in_psum, flags_ready = sem("lo_sums_ready"), sem("flags_in_psum"), sem("flags_ready")
        chain = sem("vector_chain")
        x1_shifted, y_centred = sem("x1_shifted"), sem("y_centred")
        var_ready = [sem(f"var_ready{i}") for i in range(4)]
        rstd_ready = [sem(f"rstd_ready{i}") for i in range(4)]
        xn_ready, xT_in_psum, xT_hi_ready, xT_ready = sem("xn_ready"), sem("xT_in_psum"), sem("xT_hi_ready"), sem("xT_ready")
        gT_in_psum, gT_hi_ready, gT_ready = sem("gT_in_psum"), sem("gT_hi_ready"), sem("gT_ready")
        v_in_psum, v_hi_ready, v_ready = sem("v_in_psum"), sem("v_hi_ready"), sem("v_ready")
        scores_ready, max_ready, probs_ready, sums_ready = sem("scores_ready"), sem("max_ready"), sem("probs_ready"), sem("sums_ready")
        pT_in_psum, pT_hi_ready, pT_ready = sem("pT_in_psum"), sem("pT_hi_ready"), sem("pT_ready")
        oT_in_psum, oT_ready = sem("oT_in_psum"), sem("oT_ready")
        o_in_psum, x1_ready, xn2_ready = sem("o_in_psum"), sem("x1_ready"), sem("xn2_ready")
        x2T_in_psum, x2T_hi_ready, x2T_ready = sem("x2T_in_psum"), sem("x2T_hi_ready"), sem("x2T_ready")
        up_in_psum, silu_ready, a1_full, a1_hi_ready, a1_lo_dve = sem("up_in_psum"), sem("silu_ready"), sem("a1_full"), sem("a1_hi_ready"), sem("a1_lo_dve")
        a1_lo_pool = sem("a1_lo_pool")
        h1_in_psum, a2_full, a2_hi_ready, a2_lo_pool, a2_lo_dve = (
            sem("h1_in_psum"), sem("a2_full"), sem("a2_hi_ready"), sem("a2_lo_pool"), sem("a2_lo_dve"))
        h2_in_psum, a3_full, a3_hi_ready, a3_lo_pool, a3_lo_dve = (
            sem("h2_in_psum"), sem("a3_full"), sem("a3_hi_ready"), sem("a3_lo_pool"), sem("a3_lo_dve"))
        yT_in_psum, yT_ready, y_in_psum = sem("yT_in_psum"), sem("yT_ready"), sem("y_in_psum")
        y_shift_ready, yn_ready, out_ready, out_stored = sem("y_shift_ready"), sem("yn_ready"), sem("out_ready"), sem("out_stored")

        def on_pool(b, slices):
            return slices - (b == LAST)

        def a1_lo_done(b, o):
            return (a1_lo_pool, POOL_A1 * b + o + 1) if o < POOL_A1 else (a1_lo_dve, (KT - POOL_A1) * b + o - POOL_A1 + 1)

        def a2_lo_done(b, o):
            return (a2_lo_pool, POOL_A2 * b + o + 1) if o < on_pool(b, POOL_A2) else (a2_lo_dve, (KT - POOL_A2) * b + o - on_pool(b, POOL_A2) + 1)

        def a3_lo_done(b, o):
            return (a3_lo_pool, POOL_A3 * b + o + 1) if o < on_pool(b, POOL_A3) else (a3_lo_dve, (KT - POOL_A3) * b + o - on_pool(b, POOL_A3) + 1)

        block = ctx.enter_context(nc.Block())

        @block.sync
        def _(sp):
            def load_x(b):
                sp.dma_start(xs[:, TB * b:TB * (b + 1), :].rearrange("p (g j) d -> p g (j d)", j=2),
                             x_view[:, 2 * b:2 * b + 2, :]).then_inc(x_loaded[b], 16)

            load_x(0)
            sp.dma_start(wa_raw[:, :], w_attn).then_inc(wa_loaded, 16)
            load_x(1)
            sp.dma_start(w12_raw[:, :], w12).then_inc(w12_loaded, 16)
            sp.dma_start(sc[:, :], scales).then_inc(sc_loaded, 16)
            sp.dma_start(h1_raw[:, :, :], h1.rearrange("(k p) o -> p k o", p=P)).then_inc(h1_loaded, 16)
            load_x(2)
            sp.dma_start(h2_raw[:, :, :], h2.rearrange("(k p) o -> p k o", p=P)).then_inc(h2_loaded, 16)
            load_x(3)
            sp.dma_start(w3_raw[:, :], w3).then_inc(w3_loaded, 16)
            for b in range(LAST):
                sp.wait_ge(out_ready, b + 1)
                sp.dma_start(out_view[:, 2 * b:2 * b + 2, :],
                             outs[:, TB * b:TB * (b + 1), :].rearrange("p (g j) d -> p g (j d)", j=2)).then_inc(out_stored, 16)
            for g in range(2):
                sp.wait_ge(out_ready, BLOCKS + g)
                sp.dma_start(out_view[:, 2 * LAST + g, :],
                             outs[:, TB * LAST + 2 * g:TB * LAST + 2 * g + 2, :].rearrange("p j d -> p (j d)")).then_inc(out_stored, 16)
            sp.wait_ge(out_stored, 16 * (BLOCKS + 1))

        @block.gpsimd
        def _(pool):
            nc.gpsimd.memset(warm[:, :], 0.0).then_inc(warm_ready, 1)
            nc.gpsimd.memset(ident[:, :], 0.0).then_inc(zeroed, 1)
            nc.gpsimd.memset(minus_half[:, :], -0.5).then_inc(zeroed, 1)
            nc.gpsimd.memset(ones[:, :], 1.0).then_inc(zeroed, 1)
            pool.wait_ge(zeroed, 3)
            nc.gpsimd.affine_select(out=ident[:, :], in_=ident[:, :], compare_op=ALU.not_equal, fill=1.0, base=0,
                                    pattern=[[-1, P]], channel_multiplier=1).then_inc(ident_ready, 1)

            def rsqrt(ln, b):
                pool.wait_ge(var_ready[ln], b + 1)
                nc.gpsimd.tensor_tensor(rstd[:, ln, :], ve[:, ln, :], minus_half[:, :], ALU.pow).then_inc(rstd_ready[ln], 1)

            def lo_part(b, o, dst, hi, hi_sem, full_sem, done):
                pool.wait_ge(hi_sem, KT * b + o + 1)
                pool.wait_ge(full_sem, KT * b + o + 1)
                nc.gpsimd.tensor_tensor(dst[:, o, :], act_full[:, o, :], hi[:, o, :].bitcast(f32), ALU.subtract).then_inc(done, 1)

            def last_add(b):
                pool.wait_ge(yn_ready, TB * (b + 1))
                pool.wait_ge(x1_ready, b + 1)
                nc.gpsimd.tensor_tensor(outs[:, TB * b:TB * (b + 1), :], y_n[:, :, :],
                                        x1[:, TB * b:TB * (b + 1), :], ALU.add).then_inc(out_ready, 1)

            def weights_lo(lo, raw, hi, split, n, done):
                pool.wait_ge(split, n)
                nc.gpsimd.tensor_tensor(lo, raw, hi.bitcast(f32), ALU.subtract).then_inc(done, 1)

            def h2_weights_lo(slices):
                for k in slices:
                    weights_lo(h2_lo[:, k, :], h2_raw[:, k, :], h2_hi[:, k, :], h2_split, k + 1, h2_ready)

            rsqrt(LN_X, 0)
            weights_lo(w12_lo[:, :], w12_raw[:, :], w12_hi[:, :], w12_split, 1, w12_ready)
            rsqrt(LN_X, 1)
            for k in range(KT):
                weights_lo(h1_lo[:, k, :], h1_raw[:, k, :], h1_hi[:, k, :], h1_split, k + 1, h1_ready)
            rsqrt(LN_O, 0)
            h2_weights_lo((0, 1))
            rsqrt(LN_X1, 0)
            h2_weights_lo((2, 3))
            weights_lo(w3_lo[:, :], w3_raw[:, :], w3_hi[:, :], w3_split, 1, w3_ready)
            for o in range(POOL_A1):
                lo_part(0, o, a1_lo, a1_hi, a1_hi_ready, a1_full, a1_lo_pool)
            rsqrt(LN_X, 2)
            for b in range(BLOCKS):
                if b > 0:
                    rsqrt(LN_Y, b - 1)
                for o in range(on_pool(b, POOL_A2)):
                    lo_part(b, o, a2_lo, a2_hi, a2_hi_ready, a2_full, a2_lo_pool)
                if b + 1 < BLOCKS:
                    rsqrt(LN_O, b + 1)
                if b + 3 < BLOCKS:
                    rsqrt(LN_X, b + 3)
                if b + 1 < BLOCKS:
                    rsqrt(LN_X1, b + 1)
                if b > 0:
                    last_add(b - 1)
                for o in range(on_pool(b, POOL_A3)):
                    lo_part(b, o, a3_lo, a3_hi, a3_hi_ready, a3_full, a3_lo_pool)
                if b + 1 < BLOCKS:
                    for o in range(POOL_A1):
                        lo_part(b + 1, o, a1_lo, a1_hi, a1_hi_ready, a1_full, a1_lo_pool)
            for g in range(2):
                pool.wait_ge(var_ready[LN_Y], BLOCKS + g)
                nc.gpsimd.tensor_tensor(rstd[:, LN_Y, 2 * g:2 * g + 2], ve[:, LN_Y, 2 * g:2 * g + 2],
                                        minus_half[:, 0:2], ALU.pow).then_inc(rstd_ready[LN_Y], 1)

        @block.scalar
        def _(act):
            def hi_from_psum(dst, src, ready, n, done):
                act.wait_ge(ready, n)
                nc.scalar.activation(dst, src, ACT.Copy).then_inc(done, 1)

            def exps(b):
                for t in range(TB):
                    g, j = divmod(t, 2)
                    if j == 0:
                        act.wait_ge(max_ready, 2 * b + g + 1)
                    if b > 0 and t == 0:
                        act.wait_ge(pT_in_psum, 2 * b)
                        act.wait_ge(x1_ready, b)
                    nc.scalar.activation(probs[:, t, :], S_BANK[g][:, j * SEQ:(j + 1) * SEQ], ACT.Exp,
                                         bias=neg_max[:, t:t + 1], accum_out=sums[:, t:t + 1]).then_inc(probs_ready, 1)

            def front(b, part):
                if part == 0:
                    if b > 0:
                        act.wait_ge(scores_ready, 2 * b)
                    hi_from_psum(xT_hi[:, :], A[1][:, :], xT_in_psum, b + 1, xT_hi_ready)
                else:
                    hi_from_psum(gT_hi[:, :], A[1][:, :], gT_in_psum, b + 1, gT_hi_ready)
                    if b > 0:
                        act.wait_ge(oT_in_psum, b)
                    hi_from_psum(v_hi[:, :, :], A[2][:, :], v_in_psum, b + 1, v_hi_ready)

            def probs_hi(b):
                for g in range(2):
                    if b > 0 and g == 0:
                        act.wait_ge(oT_in_psum, b)
                    hi_from_psum(pT_hi[:, g, :], PT_BANK[g][:, :], pT_in_psum, 2 * b + g + 1, pT_hi_ready)

            def attention_T(b):
                act.wait_ge(oT_in_psum, b + 1)
                if b > 0:
                    act.wait_ge(o_in_psum, b)
                nc.scalar.activation(oT[:, :], A[0][:, :], ACT.Copy).then_inc(oT_ready, 1)

            def x2T(b):
                if b > 0:
                    act.wait_ge(up_in_psum, KT * b)
                hi_from_psum(x2T_hi[:, :], A[3][:, :], x2T_in_psum, b + 1, x2T_hi_ready)

            def silus(b, slices):
                for o in slices:
                    act.wait_ge(up_in_psum, KT * b + o + 1)
                    if KT * b + o >= 2:
                        act.wait_ge(a1_full, KT * b + o - 1)
                    nc.scalar.activation(silu1[:, o % 2, :], F[2 * (o % 2)][:, :], ACT.Silu,
                                         scale=sc[:, S_W1 + o:S_W1 + o + 1]).then_inc(silu_ready, 1)

            def gelu(b, o, first_scale, in_psum, slot_free, done):
                act.wait_ge(in_psum, KT * b + o + 1)
                act.wait_ge(*slot_free)
                nc.scalar.activation(act_full[:, o, :], F[o][:, :], ACT.Gelu,
                                     scale=sc[:, first_scale + o:first_scale + o + 1]).then_inc(done, 1)

            def gelu1(b, o):
                gelu(b, o, S_H1, h1_in_psum, a1_lo_done(b, o), a2_full)

            def gelu2(b, o):
                gelu(b, o, S_H2, h2_in_psum, a2_lo_done(b, o), a3_full)

            def scaled_yT(b):
                act.wait_ge(yT_in_psum, b + 1)
                if b > 0:
                    act.wait_ge(y_in_psum, b)
                nc.scalar.activation(yT[:, :], A[1][:, :], ACT.Copy, scale=sc[:, S_W3:S_W3 + 1]).then_inc(yT_ready, 1)

            def y_normalised(b):
                act.wait_ge(y_shift_ready, b + 1)
                if b > 0:
                    act.wait_ge(out_ready, b)
                for t in range(TB):
                    nc.scalar.activation(y_n[:, t, :], A[2][:, t * D:(t + 1) * D], ACT.Identity,
                                         bias=y_shift[:, t:t + 1], scale=rstd[:, LN_Y, t:t + 1]).then_inc(yn_ready, 1)

            def weights_hi(dst, raw, loaded, split):
                act.wait_ge(loaded, 16)
                nc.scalar.activation(dst, raw, ACT.Copy).then_inc(split, 1)

            def sum_of_lo(n, lo, ready, count):
                act.wait_ge(ready, count)
                if n > 0:
                    act.wait_ge(lo_sums_ready, n)
                nc.scalar.activation(lo_abs[:, 0:LO_COLUMNS[n]], lo, ACT.Abs,
                                     accum_out=lo_sums[:, n:n + 1]).then_inc(lo_sums_ready, 1)

            LO_COLUMNS = (2 * HID, KT * HID, KT * HID, KT * D)
            S_BANK = (A[3], A[0])
            PT_BANK = (A[3], A[1])

            act.wait_ge(qk_summed, 1)
            nc.scalar.activation(qk[:, :], F[0][:, 0:D], ACT.Copy, scale=SCALE).then_inc(qk_copied, 1)
            act.wait_ge(sc_loaded, 16)
            def h1_weights_hi(slices):
                for k in slices:
                    weights_hi(h1_hi[:, k, :], h1_raw[:, k, :], h1_loaded, h1_split)

            front(0, 0)
            weights_hi(w12_hi[:, :], w12_raw[:, :], w12_loaded, w12_split)
            front(0, 1)
            h1_weights_hi((0, 1))
            exps(0)
            probs_hi(0)
            h1_weights_hi((2,))
            attention_T(0)
            front(1, 0)
            h1_weights_hi((3,))
            sum_of_lo(W12, w12_lo[:, :], w12_ready, 1)
            for k in range(KT):
                weights_hi(h2_hi[:, k, :], h2_raw[:, k, :], h2_loaded, h2_split)
            front(1, 1)
            sum_of_lo(H1, h1_lo[:, :, :].rearrange("p k o -> p (k o)"), h1_ready, KT)
            weights_hi(w3_hi[:, :], w3_raw[:, :], w3_loaded, w3_split)
            x2T(0)
            silus(0, range(KT))
            sum_of_lo(H2, h2_lo[:, :, :].rearrange("p k o -> p (k o)"), h2_ready, KT)
            sum_of_lo(W3, w3_lo[:, :], w3_ready, 1)
            for b in range(BLOCKS):
                if b + 1 < BLOCKS:
                    exps(b + 1)
                    probs_hi(b + 1)
                gelu1(b, 0)
                gelu1(b, 1)
                if b + 1 < BLOCKS:
                    attention_T(b + 1)
                gelu1(b, 2)
                gelu1(b, 3)
                if b + 2 < BLOCKS:
                    front(b + 2, 0)
                if b > 0:
                    y_normalised(b - 1)
                gelu2(b, 0)
                gelu2(b, 1)
                gelu2(b, 2)
                if b + 2 < BLOCKS:
                    front(b + 2, 1)
                if b + 2 < BLOCKS:
                    x2T(b + 1)
                    gelu2(b, 3)
                elif b < LAST:
                    gelu2(b, 3)
                    x2T(b + 1)
                if b + 1 < BLOCKS:
                    silus(b + 1, (0, 1))
                if b < LAST:
                    scaled_yT(b)
                    silus(b + 1, (2, 3))
            for g in range(2):
                c = slice(g * SEQ, (g + 1) * SEQ)
                act.wait_ge(h2_in_psum, KT * BLOCKS + g)
                if g == 0:
                    act.wait_ge(*a2_lo_done(LAST, KT - 1))
                nc.scalar.activation(act_full[:, KT - 1, c], (F[3], A[3])[g][:, c], ACT.Gelu,
                                     scale=sc[:, S_H2 + KT - 1:S_H2 + KT]).then_inc(a3_full, 1)
            for g in range(2):
                c = slice(g * SEQ, (g + 1) * SEQ)
                act.wait_ge(yT_in_psum, BLOCKS + g)
                if g == 0:
                    act.wait_ge(y_in_psum, LAST)
                nc.scalar.activation(yT[:, c], A[(1, 0)[g]][:, c], ACT.Copy, scale=sc[:, S_W3:S_W3 + 1]).then_inc(yT_ready, 1)

        @block.vector
        def _(dve):
            links = [0]

            def link(ins):
                links[0] += 1
                ins.then_inc(chain, 1)
                dve.wait_ge(chain, links[0])

            def lo_part(dst, full, hi, hi_sem, n, done):
                dve.wait_ge(hi_sem, n)
                nc.vector.tensor_tensor(dst, full, hi.bitcast(f32), ALU.subtract).then_inc(done, 1)

            def statistics(ln, tiles):
                for t in range(TB):
                    last = nc.vector.bn_stats(stats[:, ln, t, :], tiles(t))
                link(last)
                for t in range(TB):
                    last = nc.vector.bn_aggr(mv[:, ln, t, :], stats[:, ln, t, :])
                link(last)

            def x_statistics(b):
                dve.wait_ge(x_loaded[b], 16)
                statistics(LN_X, lambda t: xs[:, TB * b + t, :])
                nc.vector.tensor_scalar(ve[:, LN_X, :], mv[:, LN_X, :, 1], EPS, None, ALU.add).then_inc(var_ready[LN_X], 1)

            def x_normalised(b):
                if b > 0:
                    dve.wait_ge(xT_in_psum, b)
                normalise(b, LN_X, lambda t: xs[:, TB * b + t, :], xn, xn_ready)

            def normalise(b, ln, src, dst, done):
                dve.wait_ge(rstd_ready[ln], b + 1)
                for t in range(TB):
                    nc.vector.tensor_scalar(dst[:, t, :], src(t), mv[:, ln, t, 0:1], rstd[:, ln, t:t + 1],
                                            ALU.subtract, ALU.mult).then_inc(done, 1)

            def maxima(b, batches):
                for g in batches:
                    s = (A[3], A[0])[g]
                    dve.wait_ge(scores_ready, 2 * b + g + 1)
                    if b > 0 and g == 0:
                        dve.wait_ge(probs_ready, TB * b)
                    nc.vector.tensor_reduce(neg_max[:, 2 * g:2 * g + 2], s[:, :].rearrange("p (j m) -> p j m", j=2),
                                            AX, ALU.max, negate=True).then_inc(max_ready, 1)

            def xT_part(b):
                lo_part(xT_lo[:, :], A[1][:, :], xT_hi[:, :], xT_hi_ready, b + 1, xT_ready)

            def gv_part(b):
                lo_part(gT_lo[:, :], A[1][:, :], gT_hi[:, :], gT_hi_ready, b + 1, gT_ready)
                lo_part(v_lo[:, :, :], A[2][:, :].rearrange("p (t d) -> p t d", t=TB), v_hi[:, :, :], v_hi_ready, b + 1, v_ready)

            def probs_lo(b):
                dve.wait_ge(probs_ready, TB * (b + 1))
                nc.vector.scalar_tensor_tensor(eps_s2[:, :], sums[:, :], EPS, sums[:, :], ALU.mult, ALU.mult).then_inc(sums_ready, 1)
                for g, s in enumerate((A[3], A[1])):
                    lo_part(pT_lo[:, g, :], s[:, :], pT_hi[:, g, :], pT_hi_ready, 2 * b + g + 1, pT_ready)

            def attention_out(b):
                dve.wait_ge(o_in_psum, b + 1)
                o = lambda t: A[3][:, t * D:(t + 1) * D]
                statistics(LN_O, o)
                dve.wait_ge(sums_ready, b + 1)
                nc.vector.tensor_tensor(ve[:, LN_O, :], mv[:, LN_O, :, 1], eps_s2[:, :], ALU.add).then_inc(var_ready[LN_O], 1)

            def x1_block(b):
                o = lambda t: A[3][:, t * D:(t + 1) * D]
                dve.wait_ge(rstd_ready[LN_O], b + 1)
                for t in range(TB):
                    last = nc.vector.scalar_tensor_tensor(x1[:, TB * b + t, :], o(t), rstd[:, LN_O, t:t + 1], xs[:, TB * b + t, :],
                                                          ALU.mult, ALU.add)
                last.then_inc(x1_ready, 1)
                nc.vector.tensor_tensor(o_shift[:, TB * b:TB * (b + 1)], mv[:, LN_O, :, 0], rstd[:, LN_O, :], ALU.mult)
                dve.wait_ge(x1_ready, b + 1)
                x1t = lambda t: x1[:, TB * b + t, :]
                statistics(LN_X1, x1t)
                nc.vector.tensor_scalar(ve[:, LN_X1, :], mv[:, LN_X1, :, 1], EPS, None, ALU.add).then_inc(var_ready[LN_X1], 1)

            def x1_normalised(b):
                if b > 0:
                    dve.wait_ge(x2T_in_psum, b)
                normalise(b, LN_X1, lambda t: x1[:, TB * b + t, :], xn2, xn2_ready)

            def x2T_part(b):
                lo_part(x2T_lo[:, :], A[3][:, :], x2T_hi[:, :], x2T_hi_ready, b + 1, x2T_ready)

            def gated(b, o):
                dve.wait_ge(silu_ready, KT * b + o + 1)
                if b > 0:
                    dve.wait_ge(*a3_lo_done(b - 1, o))
                nc.vector.scalar_tensor_tensor(act_full[:, o, :], F[2 * (o % 2) + 1][:, :], sc[:, S_W2 + o:S_W2 + o + 1],
                                               silu1[:, o % 2, :], ALU.mult, ALU.mult).then_inc(a1_full, 1)
                act_hi(b, o, a1_hi, a1_full, a1_hi_ready, h1_in_psum, KT * b)

            def act_hi(b, o, hi, full_sem, hi_sem, used_sem, used):
                if b > 0 and o == 0:
                    dve.wait_ge(used_sem, used)
                dve.wait_ge(full_sem, KT * b + o + 1)
                nc.vector.tensor_copy(hi[:, o, :], act_full[:, o, :]).then_inc(hi_sem, 1)

            def a2_parts(b, o):
                act_hi(b, o, a2_hi, a2_full, a2_hi_ready, h2_in_psum, KT * b)
                if o >= on_pool(b, POOL_A2):
                    act_lo(b, o, a2_lo, a2_hi, a2_hi_ready, a2_full, a2_lo_dve)

            def a3_parts(b, o):
                act_hi(b, o, a3_hi, a3_full, a3_hi_ready, yT_in_psum, b)
                if o >= on_pool(b, POOL_A3):
                    act_lo(b, o, a3_lo, a3_hi, a3_hi_ready, a3_full, a3_lo_dve)

            def last_a3_parts(g):
                o, c, n = KT - 1, slice(g * SEQ, (g + 1) * SEQ), KT * BLOCKS + g
                dve.wait_ge(a3_full, n)
                nc.vector.tensor_copy(a3_hi[:, o, c], act_full[:, o, c]).then_inc(a3_hi_ready, 1)
                lo_part(a3_lo[:, o, c], act_full[:, o, c], a3_hi[:, o, c], a3_hi_ready, n, a3_lo_dve)

            def act_lo(b, o, dst, hi, hi_sem, full_sem, done):
                dve.wait_ge(full_sem, KT * b + o + 1)
                lo_part(dst[:, o, :], act_full[:, o, :], hi[:, o, :], hi_sem, KT * b + o + 1, done)

            def gates(b, slices):
                for o in slices:
                    gated(b, o)
                for o in slices:
                    if o >= POOL_A1:
                        act_lo(b, o, a1_lo, a1_hi, a1_hi_ready, a1_full, a1_lo_dve)

            def y_statistics(b):
                dve.wait_ge(y_in_psum, b + 1)
                if b > 0:
                    dve.wait_ge(yn_ready, TB * b)
                statistics(LN_Y, lambda t: A[2][:, t * D:(t + 1) * D])
                nc.vector.tensor_scalar(ve[:, LN_Y, :], mv[:, LN_Y, :, 1], EPS, None, ALU.add).then_inc(var_ready[LN_Y], 1)

            def y_shifts(b):
                dve.wait_ge(rstd_ready[LN_Y], b + 1)
                link(nc.vector.tensor_tensor(y_shift[:, :], mv[:, LN_Y, :, 0], rstd[:, LN_Y, :], ALU.mult))
                nc.vector.scalar_tensor_tensor(y_shift[:, :], y_shift[:, :], -1.0, o_shift[:, TB * b:TB * (b + 1)],
                                               ALU.mult, ALU.subtract).then_inc(y_shift_ready, 1)

            def shift_x1(b):
                for t in range(TB):
                    nc.vector.tensor_scalar(x1[:, TB * b + t, :], x1[:, TB * b + t, :], o_shift[:, TB * b + t:TB * b + t + 1],
                                            None, ALU.subtract).then_inc(x1_shifted, 1)

            def last_statistics(g):
                y = lambda t: (A[2], F[0])[g][:, t * D:(t + 1) * D]
                tiles = (2 * g, 2 * g + 1)
                dve.wait_ge(y_in_psum, BLOCKS + g)
                for t in tiles:
                    last = nc.vector.bn_stats(stats[:, LN_Y, t, :], y(t))
                link(last)
                for t in tiles:
                    last = nc.vector.bn_aggr(mv[:, LN_Y, t, :], stats[:, LN_Y, t, :])
                link(last)
                c = slice(2 * g, 2 * g + 2)
                nc.vector.tensor_scalar(ve[:, LN_Y, c], mv[:, LN_Y, c, 1], EPS, None, ALU.add).then_inc(var_ready[LN_Y], 1)

            def last_centred(g):
                y = lambda t: (A[2], F[0])[g][:, t * D:(t + 1) * D]
                for t in (2 * g, 2 * g + 1):
                    last = nc.vector.tensor_scalar(outs[:, TB * LAST + t, :], y(t), mv[:, LN_Y, t, 0:1], None, ALU.subtract)
                last.then_inc(y_centred, 1)

            def last_out(g):
                dve.wait_ge(rstd_ready[LN_Y], BLOCKS + g)
                dve.wait_ge(y_centred, g + 1)
                dve.wait_ge(x1_shifted, TB)
                for t in (2 * g, 2 * g + 1):
                    last = nc.vector.scalar_tensor_tensor(outs[:, TB * LAST + t, :], outs[:, TB * LAST + t, :], rstd[:, LN_Y, t:t + 1],
                                                          x1[:, TB * LAST + t, :], ALU.mult, ALU.add)
                last.then_inc(out_ready, 1)

            def copy_flags(group, source):
                dve.wait_ge(flags_in_psum, group + 1)
                c = slice(*FLAG_GROUPS[group])
                nc.vector.tensor_copy(flags[0:1, c], source[0:1, c]).then_inc(flags_ready, 1)

            x_statistics(0)
            dve.wait_ge(wa_loaded, 16)
            nc.vector.tensor_copy(wv_hi[:, :], wa_raw[:, 2 * D:3 * D]).then_inc(wv_split, 1)
            lo_part(wv_lo[:, :], wa_raw[:, 2 * D:3 * D], wv_hi[:, :], wv_split, 1, wv_ready)
            x_normalised(0)
            dve.wait_ge(qk_copied, 1)
            nc.vector.tensor_copy(qk_hi[:, :], qk[:, :]).then_inc(qk_split, 1)
            lo_part(qk_lo[:, :], qk[:, :], qk_hi[:, :], qk_split, 1, qk_ready)
            xT_part(0)
            x_statistics(1)
            gv_part(0)
            maxima(0, (0, 1))
            probs_lo(0)
            x_normalised(1)
            attention_out(0)
            xT_part(1)
            x1_block(0)
            gv_part(1)
            x1_normalised(0)
            copy_flags(0, F[0])
            x2T_part(0)
            gates(0, (0, 1))
            gates(0, (2, 3))
            maxima(1, (0, 1))
            x_statistics(2)
            for b in range(BLOCKS):
                if b > 0:
                    y_statistics(b - 1)
                if b + 1 < BLOCKS:
                    probs_lo(b + 1)
                if b > 0:
                    y_shifts(b - 1)
                if b == LAST:
                    shift_x1(b)
                if b == 0:
                    copy_flags(1, A[2])
                if b + 2 < BLOCKS:
                    x_normalised(b + 2)
                for o in range(2):
                    a2_parts(b, o)
                if b + 3 < BLOCKS:
                    x_statistics(b + 3)
                a2_parts(b, 2)
                if b + 1 < BLOCKS:
                    attention_out(b + 1)
                a2_parts(b, 3)
                if b + 2 < BLOCKS:
                    xT_part(b + 2)
                if b + 1 < BLOCKS:
                    x1_block(b + 1)
                a3_parts(b, 0)
                if b + 1 < BLOCKS:
                    x1_normalised(b + 1)
                a3_parts(b, 1)
                a3_parts(b, 2)
                if b + 2 < BLOCKS:
                    gv_part(b + 2)
                if b + 1 < BLOCKS:
                    x2T_part(b + 1)
                if b < LAST:
                    a3_parts(b, 3)
                else:
                    last_a3_parts(0)
                    last_a3_parts(1)
                if b + 1 < BLOCKS:
                    gates(b + 1, (0, 1))
                if b + 2 < BLOCKS:
                    maxima(b + 2, (0,))
                if b + 1 < BLOCKS:
                    gates(b + 1, (2, 3))
                if b + 2 < BLOCKS:
                    maxima(b + 2, (1,))
            for step in (last_statistics, last_centred, last_out):
                for g in range(2):
                    step(g)

        @block.tensor
        def _(pe):
            def product(out, terms):
                last = None
                for n, (w_hi, w_lo, x_hi, x_lo) in enumerate(terms):
                    for m, (w, v) in enumerate(((w_hi, x_hi), (w_hi, x_lo), (w_lo, x_hi))):
                        last = nc.tensor.matmul(out, w, v, start=(n == 0 and m == 0), stop=(n == len(terms) - 1 and m == 2))
                return last

            def ffn_product(n, groups, hi_ready=None, lo_ready=None):
                last_slice = len(groups[0][1]) - 1
                for k in range(last_slice + 1):
                    if hi_ready:
                        pe.wait_ge(*hi_ready(k))
                    for out, terms in groups:
                        nc.tensor.matmul(out, terms[k][0], terms[k][2], start=(k == 0), stop=False)
                with pe.If(flag[n] != 0):
                    for out, terms in groups:
                        for _, w_lo, x_hi, _ in terms:
                            nc.tensor.matmul(out, w_lo, x_hi, start=False, stop=False)
                last = []
                for i, (out, terms) in enumerate(groups):
                    for k, (w_hi, _, _, x_lo) in enumerate(terms):
                        if lo_ready and i == 0:
                            pe.wait_ge(*lo_ready(k))
                        mm = nc.tensor.matmul(out, w_hi, x_lo, start=False, stop=(k == last_slice))
                    last.append(mm)
                return last

            def sum_flags(group, out):
                pe.wait_ge(lo_sums_ready, FLAG_GROUPS[group][1])
                c = slice(*FLAG_GROUPS[group])
                nc.tensor.matmul(out[0:1, c], ones[:, :], lo_sums[:, c], start=True, stop=True).then_inc(flags_in_psum, 1)

            def read_flag(n):
                pe.wait_ge(flags_ready, (1, 1, 2, 2)[n])
                flag[n] = pe.value_load(flags[0:1, n:n + 1].bitcast(mybir.dt.int32))

            flag = {}

            def front_transposes(b):
                if b > 0:
                    pe.wait_ge(pT_ready, 2 * b)
                for t in range(TB):
                    pe.wait_ge(xn_ready, TB * b + t + 1)
                    last = nc.tensor.transpose(A[1][:, t * P:(t + 1) * P], xn[:, t, :], ident[:, :])
                last.then_inc(xT_in_psum, 1)

            def front_projections(b):
                pe.wait_ge(xT_ready, b + 1)
                if b == 0:
                    pe.wait_ge(qk_ready, 1)
                    pe.wait_ge(wv_ready, 1)
                product(A[1][:, :], [(qk_hi[:, :], qk_lo[:, :], xT_hi[:, :], xT_lo[:, :])]).then_inc(gT_in_psum, 1)
                if b >= 3:
                    pe.wait_ge(yn_ready, TB * (b - 2))
                for t in range(TB):
                    c = slice(t * P, (t + 1) * P)
                    last = product(A[2][:, c], [(xT_hi[:, c], xT_lo[:, c], wv_hi[:, :], wv_lo[:, :])])
                last.then_inc(v_in_psum, 1)

            def front_scores(b, batches):
                pe.wait_ge(gT_ready, b + 1)
                if b > 0:
                    pe.wait_ge(x2T_ready, b)
                    pe.wait_ge(oT_ready, b)
                for g in batches:
                    s = (A[3], A[0])[g]
                    keys = slice(g * SEQ, (g + 1) * SEQ)
                    for j in range(2):
                        c = slice((2 * g + j) * P, (2 * g + j + 1) * P)
                        last = product(s[:, j * SEQ:(j + 1) * SEQ], [(gT_hi[:, c], gT_lo[:, c], xT_hi[:, keys], xT_lo[:, keys])])
                    last.then_inc(scores_ready, 1)

            def probs_transposes(b):
                for g, s in enumerate((A[3], A[1])):
                    pe.wait_ge(probs_ready, TB * b + 2 * g + 2)
                    if g == 0:
                        pe.wait_ge(ident_ready, 1)
                    elif b >= 2:
                        pe.wait_ge(yT_ready, b - 1)
                    elif b == 0:
                        pe.wait_ge(gT_ready, 1)
                    for h in range(2):
                        for j in range(2):
                            c = (2 * h + j) * P
                            last = nc.tensor.transpose(s[:, c:c + P], probs[:, 2 * g + j, h * P:(h + 1) * P], ident[:, :])
                    last.then_inc(pT_in_psum, 1)

            def attend(b):
                pe.wait_ge(v_ready, b + 1)
                for g in range(2):
                    pe.wait_ge(pT_ready, 2 * b + g + 1)
                    last = product(A[0][:, g * SEQ:(g + 1) * SEQ],
                                   [(v_hi[:, 2 * g + h, :], v_lo[:, 2 * g + h, :],
                                     pT_hi[:, g, h * SEQ:(h + 1) * SEQ], pT_lo[:, g, h * SEQ:(h + 1) * SEQ]) for h in range(2)])
                last.then_inc(oT_in_psum, 1)

            def attention_transposes(b):
                pe.wait_ge(oT_ready, b + 1)
                for t in range(TB):
                    last = nc.tensor.transpose(A[3][:, t * P:(t + 1) * P], oT[:, t * P:(t + 1) * P], ident[:, :])
                last.then_inc(o_in_psum, 1)

            def x2_transposes(b):
                for t in range(TB):
                    pe.wait_ge(xn2_ready, TB * b + t + 1)
                    last = nc.tensor.transpose(A[3][:, t * P:(t + 1) * P], xn2[:, t, :], ident[:, :])
                last.then_inc(x2T_in_psum, 1)

            def up(b, slices):
                pe.wait_ge(x2T_ready, b + 1)
                for o in slices:
                    if o >= 2:
                        pe.wait_ge(a1_full, KT * b + o - 1)
                    elif b > 0:
                        pe.wait_ge(a3_full, KT * (b - 1) + 2 * o + 2)
                    columns = [slice(m * HID + o * P, m * HID + (o + 1) * P) for m in range(2)]
                    ffn_product(W12, [(F[2 * (o % 2) + m][:, :], [(w12_hi[:, c], w12_lo[:, c], x2T_hi[:, :], x2T_lo[:, :])])
                                      for m, c in enumerate(columns)])[-1].then_inc(up_in_psum, 1)

            def hidden(b, slices, flag_n, w_hi, w_lo, x_hi, x_lo, bank_free, hi_sem, lo_done, done):
                groups = []
                for o in slices:
                    pe.wait_ge(*bank_free(o))
                    c = slice(o * P, (o + 1) * P)
                    groups.append((F[o][:, :], [(w_hi[:, k, c], w_lo[:, k, c], x_hi[:, k, :], x_lo[:, k, :]) for k in range(KT)]))
                first = slices[0] == 0
                for last in ffn_product(flag_n, groups, (lambda k: (hi_sem, KT * b + k + 1)) if first else None,
                                        (lambda k: lo_done(b, k)) if first else None):
                    last.then_inc(done, 1)

            def down(b):
                pe.wait_ge(gT_ready, min(b + 3, BLOCKS))
                ffn_product(W3, [(A[1][:, :], [(w3_hi[:, k * D:(k + 1) * D], w3_lo[:, k * D:(k + 1) * D], a3_hi[:, k, :], a3_lo[:, k, :])
                                               for k in range(KT)])],
                            lambda k: (a3_hi_ready, KT * b + k + 1), lambda k: a3_lo_done(b, k))[0].then_inc(yT_in_psum, 1)

            def last_h2_slice(g):
                c, o = slice(g * SEQ, (g + 1) * SEQ), slice((KT - 1) * P, KT * P)
                pe.wait_ge(a2_full, KT * BLOCKS)
                ffn_product(H2, [((F[3], A[3])[g][:, c], [(h2_hi[:, k, o], h2_lo[:, k, o], a2_hi[:, k, c], a2_lo[:, k, c])
                                                    for k in range(KT)])])[0].then_inc(h2_in_psum, 1)

            def last_down(g):
                c = slice(g * SEQ, (g + 1) * SEQ)
                ffn_product(W3, [(A[(1, 0)[g]][:, c], [(w3_hi[:, k * D:(k + 1) * D], w3_lo[:, k * D:(k + 1) * D],
                                                        a3_hi[:, k, c], a3_lo[:, k, c]) for k in range(KT)])],
                            lambda k: (a3_hi_ready, KT * LAST + k + 1 + (g if k == KT - 1 else 0)),
                            lambda k: (a3_lo_dve, a3_lo_done(LAST, k)[1] + g) if k == KT - 1 else a3_lo_done(LAST, k),
                            )[0].then_inc(yT_in_psum, 1)

            def last_y_transposes(g):
                pe.wait_ge(yT_ready, BLOCKS + g)
                for t in (2 * g, 2 * g + 1):
                    last = nc.tensor.transpose((A[2], F[0])[g][:, t * P:(t + 1) * P], yT[:, t * P:(t + 1) * P], ident[:, :])
                last.then_inc(y_in_psum, 1)

            def y_transposes(b):
                pe.wait_ge(yT_ready, b + 1)
                pe.wait_ge(v_ready, min(b + 3, BLOCKS))
                for t in range(TB):
                    last = nc.tensor.transpose(A[2][:, t * P:(t + 1) * P], yT[:, t * P:(t + 1) * P], ident[:, :])
                last.then_inc(y_in_psum, 1)

            def h1_layer(b, slices):
                hidden(b, slices, H1, h1_hi, h1_lo, a1_hi, a1_lo, lambda o: (a1_full, KT * b + 3 + o // 2),
                       a1_hi_ready, a1_lo_done, h1_in_psum)

            def h2_layer(b, slices):
                hidden(b, slices, H2, h2_hi, h2_lo, a2_hi, a2_lo, lambda o: (a2_full, KT * b + o + 1),
                       a2_hi_ready, a2_lo_done, h2_in_psum)

            def keep_warm(n):
                for _ in range(n):
                    nc.tensor.matmul(F[3][:, :], warm[:, 0:P], warm[:, :], start=True, stop=True)

            pe.wait_ge(warm_ready, 1)
            keep_warm(WARM[0])
            pe.wait_ge(wa_loaded, 16)
            nc.tensor.matmul(F[0][:, 0:D], wa_raw[:, 0:D], wa_raw[:, D:2 * D], start=True, stop=True).then_inc(qk_summed, 1)
            pe.wait_ge(ident_ready, 1)
            keep_warm(WARM[1])
            front_transposes(0)
            keep_warm(WARM[2])
            front_projections(0)
            front_scores(0, (0, 1))
            keep_warm(WARM[3])
            probs_transposes(0)
            keep_warm(WARM[4])
            attend(0)
            front_transposes(1)
            attention_transposes(0)
            keep_warm(WARM[5])
            front_projections(1)
            keep_warm(WARM[6])
            pe.wait_ge(qk_copied, 1)
            sum_flags(0, F[0])
            x2_transposes(0)
            read_flag(W12)
            read_flag(H1)
            keep_warm(WARM[7])
            up(0, range(KT))
            front_scores(1, (0, 1))
            for b in range(BLOCKS):
                if b > 0:
                    y_transposes(b - 1)
                h1_layer(b, (0, 1))
                if b == 0:
                    pe.wait_ge(v_ready, 2)
                    sum_flags(1, A[2])
                if b + 1 < BLOCKS:
                    probs_transposes(b + 1)
                h1_layer(b, (2,))
                if b + 1 < BLOCKS:
                    attend(b + 1)
                h1_layer(b, (3,))
                if b + 1 < BLOCKS:
                    attention_transposes(b + 1)
                if b == 0:
                    read_flag(H2)
                    read_flag(W3)
                if b + 2 < BLOCKS:
                    front_transposes(b + 2)
                h2_layer(b, (0, 1))
                h2_layer(b, (2,))
                if b + 2 < BLOCKS:
                    front_projections(b + 2)
                if b + 2 < BLOCKS:
                    x2_transposes(b + 1)
                    h2_layer(b, (3,))
                elif b < LAST:
                    h2_layer(b, (3,))
                    x2_transposes(b + 1)
                if b + 1 < BLOCKS:
                    up(b + 1, (0, 1))
                if b < LAST:
                    down(b)
                if b + 2 < BLOCKS:
                    front_scores(b + 2, (0,))
                if b + 1 < BLOCKS:
                    up(b + 1, (2, 3))
                if b + 2 < BLOCKS:
                    front_scores(b + 2, (1,))
            last_h2_slice(0)
            last_h2_slice(1)
            last_down(0)
            last_down(1)
            last_y_transposes(0)
            last_y_transposes(1)


def kernel(**inputs):
    import concourse.bacc as bacc
    from concourse.bass_utils import run_bass_kernel_spmd

    a = {name: np.asarray(value) for name, value in inputs.items()}
    w_qkv = a["L0_attn_W_qkv"]
    arrays = {
        "x": a["L0_attn_x"],
        "w_attn": np.concatenate([w_qkv[:D], w_qkv[D:2 * D], w_qkv[2 * D:].T], axis=1),
        "w12": np.concatenate([a["L0_ffn_w1_w"].T, a["L0_ffn_w2_w"].T], axis=1),
        "h1": a["L0_ffn_h1_w"].T,
        "h2": a["L0_ffn_h2_w"].T,
        "w3": a["L0_ffn_w3_w"].T.reshape(KT, P, D).transpose(1, 0, 2).reshape(P, KT * D),
        "scales": np.concatenate([a["L0_ffn_" + n].reshape(-1, P) for n in ("w1_s", "w2_s", "h1_s", "h2_s", "w3_s")]).T,
    }
    arrays = {name: np.ascontiguousarray(value) for name, value in arrays.items()}
    nc = bacc.Bacc("TRN2", target_bir_lowering=False, num_devices=1)
    args = [nc.dram_tensor(name, v.shape, mybir.dt.from_np(v.dtype), kind="ExternalInput").ap() for name, v in arrays.items()]
    out = nc.dram_tensor("out", (BATCHES, SEQ, D), mybir.dt.float32, kind="ExternalOutput").ap()
    sandwich_kernel(nc, *args, out)
    result = run_bass_kernel_spmd(nc, [arrays], core_ids=[0])
    return result.results[0]["out"]
```
